# Optimizing a Trainium2 kernel written in Bass

```python
import numpy as np
import jax
import jax.numpy as jnp

def _softmax(x, axis=-1):
    return jax.nn.softmax(x, axis=axis)
def _gelu(x):
    return jax.nn.gelu(x, approximate=True)
def _silu(x):
    return jax.nn.silu(x)
def _sigmoid(x):
    return jax.nn.sigmoid(x)
def _layernorm(x, axis=-1, eps=1e-5):
    m = jnp.mean(x, axis=axis, keepdims=True)
    v = jnp.var(x, axis=axis, keepdims=True)
    return (x - m) / jnp.sqrt(v + eps)
def _scatter_add(tgt, idx, src, axis=0):
    return tgt.at[idx].add(src)
def _segment_sum(src, seg, n):
    return jax.ops.segment_sum(src, seg, n)

kernel_name = 'mk_metaformer_d2_conv_nchw128_0a6681'

def setup_inputs(seed: int = 0):
    np.random.seed(seed)
    _w = jnp.asarray
    def _rec_inputs():
        import jax
        import jax.numpy as jnp
        _gk = jax.random.key(seed)
        x = -0.000929 + 1 * jax.random.normal(jax.random.fold_in(_gk, 1), (2, 128, 64, 64), jnp.float32)
        return x
    x = _rec_inputs()
    def _L0_conv_setup():
        import jax, jax.numpy as jnp
        import numpy as np
        GN_GROUPS = 16
        EPS = 1e-05

        def conv2d(x, w, b=None, padding=0):
            out = jax.lax.conv_general_dilated(x, w, (1, 1), [(padding, padding), (padding, padding)], dimension_numbers=('NCHW', 'OIHW', 'NCHW'))
            if b is not None:
                out = out + b[None, :, None, None]
            return out

        def group_norm(x, gamma, beta):
            B, C, H, W = x.shape
            xg = x.reshape(B, GN_GROUPS, C // GN_GROUPS, H, W)
            m = xg.mean(axis=(2, 3, 4), keepdims=True)
            v = xg.var(axis=(2, 3, 4), keepdims=True)
            xg = (xg - m) * jax.lax.rsqrt(v + EPS)
            return xg.reshape(B, C, H, W) * gamma[None, :, None, None] + beta[None, :, None, None]

        def bilinear_sample(x, py, px):
            B, C, H, W = x.shape
            y0 = jnp.floor(py)
            x0 = jnp.floor(px)
            xf = x.reshape(B, C, H * W)

            def gather(yi, xi):
                valid = (yi >= 0) & (yi <= H - 1) & (xi >= 0) & (xi <= W - 1)
                yc = jnp.clip(yi, 0, H - 1).astype(jnp.int32)
                xc = jnp.clip(xi, 0, W - 1).astype(jnp.int32)
                idx = (yc * W + xc).reshape(B, -1)
                g = jnp.take_along_axis(xf, idx[:, None, :], axis=2)
                g = g.reshape(B, C, *yi.shape[1:])
                return g * valid[:, None].astype(x.dtype)
            wy = (py - y0)[:, None]
            wx = (px - x0)[:, None]
            v00 = gather(y0, x0)
            v01 = gather(y0, x0 + 1)
            v10 = gather(y0 + 1, x0)
            v11 = gather(y0 + 1, x0 + 1)
            return v00 * (1 - wy) * (1 - wx) + v01 * (1 - wy) * wx + v10 * wy * (1 - wx) + v11 * wy * wx

        def deform_conv(x, off_w, off_b, mod_w, mod_b, reg_w, k, pad):
            B, C, H, W = x.shape
            offset = conv2d(x, off_w, off_b, pad)
            mask = 2.0 * jax.nn.sigmoid(conv2d(x, mod_w, mod_b, pad))
            off = offset.reshape(B, k * k, 2, H, W)
            ky, kx = jnp.meshgrid(jnp.arange(k), jnp.arange(k), indexing='ij')
            base_y = (jnp.arange(H) - pad).astype(x.dtype)[None, None, :, None] + ky.reshape(1, -1, 1, 1).astype(x.dtype)
            base_x = (jnp.arange(W) - pad).astype(x.dtype)[None, None, None, :] + kx.reshape(1, -1, 1, 1).astype(x.dtype)
            py = base_y + off[:, :, 0]
            px = base_x + off[:, :, 1]
            sampled = bilinear_sample(x, py, px) * mask[:, None]
            O = reg_w.shape[0]
            return jnp.einsum('bckhw,ock->bohw', sampled, reg_w.reshape(O, C, k * k))

        def branch(x, off_w, off_b, mod_w, mod_b, reg_w, gng, gnb, k, pad):
            y = deform_conv(x, off_w, off_b, mod_w, mod_b, reg_w, k, pad)
            return jax.nn.relu(group_norm(y, gng, gnb))

        def _forward(x, b1_offw, b1_offb, b1_modw, b1_modb, b1_regw, b1_gng, b1_gnb, b2_offw, b2_offb, b2_modw, b2_modb, b2_regw, b2_gng, b2_gnb, b3_offw, b3_offb, b3_modw, b3_modb, b3_regw, b3_gng, b3_gnb, b4_offw, b4_offb, b4_modw, b4_modb, b4_regw, b4_gng, b4_gnb, pool_w, pool_gng, pool_gnb, fuse_w, fuse_gng, fuse_gnb):
            x1 = branch(x, b1_offw, b1_offb, b1_modw, b1_modb, b1_regw, b1_gng, b1_gnb, 1, 0)
            x2 = branch(x, b2_offw, b2_offb, b2_modw, b2_modb, b2_regw, b2_gng, b2_gnb, 1, 0)
            x3 = branch(x, b3_offw, b3_offb, b3_modw, b3_modb, b3_regw, b3_gng, b3_gnb, 3, 1)
            x4 = branch(x, b4_offw, b4_offb, b4_modw, b4_modb, b4_regw, b4_gng, b4_gnb, 7, 3)
            xm = x.mean(axis=(2, 3), keepdims=True)
            x5 = jax.nn.relu(group_norm(conv2d(xm, pool_w), pool_gng, pool_gnb))
            x5 = jnp.broadcast_to(x5, x1.shape)
            cat = jnp.concatenate([x1, x2, x3, x4, x5], axis=1)
            out = jax.nn.relu(group_norm(conv2d(cat, fuse_w), fuse_gng, fuse_gnb))
            return out
        key = jax.random.key(seed)
        keys = iter(jax.random.split(key, 64))
        C, O = (128, 256)
        inp = {}
        inp['x'] = jax.random.normal(next(keys), (2, C, 64, 64), jnp.float32)
        for name, k in [('b1', 1), ('b2', 1), ('b3', 3), ('b4', 7)]:
            inp[f'{name}_offw'] = 0.01 * jax.random.normal(next(keys), (2 * k * k, C, k, k), jnp.float32)
            inp[f'{name}_offb'] = jnp.zeros((2 * k * k,), jnp.float32)
            inp[f'{name}_modw'] = 0.01 * jax.random.normal(next(keys), (k * k, C, k, k), jnp.float32)
            inp[f'{name}_modb'] = jnp.zeros((k * k,), jnp.float32)
            inp[f'{name}_regw'] = jax.random.normal(next(keys), (O, C, k, k), jnp.float32) / np.sqrt(C * k * k)
            inp[f'{name}_gng'] = jnp.ones((O,), jnp.float32)
            inp[f'{name}_gnb'] = jnp.zeros((O,), jnp.float32)
        inp['pool_w'] = jax.random.normal(next(keys), (O, C, 1, 1), jnp.float32) / np.sqrt(C)
        inp['pool_gng'] = jnp.ones((O,), jnp.float32)
        inp['pool_gnb'] = jnp.zeros((O,), jnp.float32)
        inp['fuse_w'] = jax.random.normal(next(keys), (C, 5 * O, 1, 1), jnp.float32) / np.sqrt(5 * O)
        inp['fuse_gng'] = jnp.ones((C,), jnp.float32)
        inp['fuse_gnb'] = jnp.zeros((C,), jnp.float32)
        return inp
    _L0_conv_all = _L0_conv_setup()
    _L0_conv_in = {k: v for k, v in _L0_conv_all.items() if k in ('b1_offw', 'b1_offb', 'b1_modw', 'b1_modb', 'b1_regw', 'b1_gng', 'b1_gnb', 'b2_offw', 'b2_offb', 'b2_modw', 'b2_modb', 'b2_regw', 'b2_gng', 'b2_gnb', 'b3_offw', 'b3_offb', 'b3_modw', 'b3_modb', 'b3_regw', 'b3_gng', 'b3_gnb', 'b4_offw', 'b4_offb', 'b4_modw', 'b4_modb', 'b4_regw', 'b4_gng', 'b4_gnb', 'pool_w', 'pool_gng', 'pool_gnb', 'fuse_w', 'fuse_gng', 'fuse_gnb', )}
    del _L0_conv_all

    def _L0_ffn_setup():
        import jax, jax.numpy as jnp
        import numpy as np
        B, N, D, C, E, K = (8, 8192, 128, 128, 8, 2)
        key = jax.random.key(seed)
        k0, k1, k2 = jax.random.split(key, 3)
        x = jax.random.normal(k0, (B, N, D), dtype=jnp.float32)
        router_w = jax.random.normal(k1, (D, E), dtype=jnp.float32) * 0.05
        router_b = jnp.zeros((E,), dtype=jnp.float32)
        expert_w = jax.random.normal(k2, (E, D, C), dtype=jnp.float32) * (1.0 / np.sqrt(D))
        expert_b = jnp.zeros((E, C), dtype=jnp.float32)
        return {'x': x, 'router_w': router_w, 'router_b': router_b, 'expert_w': expert_w, 'expert_b': expert_b}
    _L0_ffn_all = _L0_ffn_setup()
    _L0_ffn_in = {k: v for k, v in _L0_ffn_all.items() if k in ('router_w', 'router_b', 'expert_w', 'expert_b', )}
    del _L0_ffn_all

    def _L1_conv_setup():
        import jax, jax.numpy as jnp
        import numpy as np
        from jax import lax
        B, DM, H, W = (2, 128, 64, 64)
        DI = 2 * DM
        DS = 16
        DC = 4
        DTR = 8

        def silu(x):
            return x * jax.nn.sigmoid(x)
        key = jax.random.key(seed)
        ks = jax.random.split(key, 12)

        def n(k, shape, scale=0.02):
            return jax.random.normal(k, shape, jnp.float32) * scale
        dt = jnp.exp(jax.random.uniform(ks[0], (DI,), jnp.float32) * (np.log(0.1) - np.log(0.001)) + np.log(0.001))
        dt = jnp.clip(dt, 0.0001)
        inv_dt = dt + jnp.log(-jnp.expm1(-dt))
        A = jnp.tile(jnp.arange(1, DS + 1, dtype=jnp.float32)[None, :], (DI, 1))
        std = DTR ** (-0.5)
        return {'hidden_states': jax.random.normal(ks[1], (B, DM, H, W), jnp.float32), 'in_proj_w': n(ks[2], (2 * DI, DM)), 'dwconv_w': n(ks[3], (2 * DI, 1, 5, 5)), 'conv1d_w': n(ks[4], (DI, 1, DC)), 'conv1d_b': jnp.zeros((DI,), jnp.float32), 'x_proj_w': n(ks[5], (DTR + 2 * DS, DI)), 'dt_proj_w': jax.random.uniform(ks[6], (DI, DTR), jnp.float32, -std, std), 'dt_proj_b': inv_dt, 'A_log': jnp.log(A), 'D': jnp.ones((DI,), jnp.float32), 'out_proj_w': n(ks[7], (DM, DI)), 'ca_fc1_w': n(ks[8], (DI // 16, DI)), 'ca_fc2_w': n(ks[9], (DI, DI // 16)), 'sa_conv_w': n(ks[10], (1, 2, 7))}
    _L1_conv_all = _L1_conv_setup()
    _L1_conv_in = {k: v for k, v in _L1_conv_all.items() if k in ('in_proj_w', 'dwconv_w', 'conv1d_w', 'conv1d_b', 'x_proj_w', 'dt_proj_w', 'dt_proj_b', 'A_log', 'D', 'out_proj_w', 'ca_fc1_w', 'ca_fc2_w', 'sa_conv_w', )}
    del _L1_conv_all

    def _L1_ffn_setup():
        import jax, jax.numpy as jnp
        import numpy as np
        B, S, D, E, H, O, K = (512, 2048, 128, 64, 512, 128, 8)
        key = jax.random.key(seed)
        k0, k1, k2, k3 = jax.random.split(key, 4)
        x = jax.random.normal(k0, (B, S, D), dtype=jnp.float32)
        gate_w = jax.random.normal(k1, (E, D), dtype=jnp.float32) * (1.0 / np.sqrt(D))
        gate_b = jnp.zeros((E,), dtype=jnp.float32)
        weight1 = jax.random.uniform(k2, (E, D + 1, H), dtype=jnp.float32, minval=-1.0, maxval=1.0) * (1.0 / np.sqrt(D + 1))
        weight2 = jax.random.uniform(k3, (E, H + 1, O), dtype=jnp.float32, minval=-1.0, maxval=1.0) * (1.0 / np.sqrt(H + 1))
        return {'x': x, 'gate_w': gate_w, 'gate_b': gate_b, 'weight1': weight1, 'weight2': weight2}
    _L1_ffn_all = _L1_ffn_setup()
    _L1_ffn_in = {k: v for k, v in _L1_ffn_all.items() if k in ('gate_w', 'gate_b', 'weight1', 'weight2', )}
    del _L1_ffn_all

    return {
        "x": x,
        "L0_conv_b1_offw": _L0_conv_in["b1_offw"],
        "L0_conv_b1_offb": _L0_conv_in["b1_offb"],
        "L0_conv_b1_modw": _L0_conv_in["b1_modw"],
        "L0_conv_b1_modb": _L0_conv_in["b1_modb"],
        "L0_conv_b1_regw": _L0_conv_in["b1_regw"],
        "L0_conv_b1_gng": _L0_conv_in["b1_gng"],
        "L0_conv_b1_gnb": _L0_conv_in["b1_gnb"],
        "L0_conv_b2_offw": _L0_conv_in["b2_offw"],
        "L0_conv_b2_offb": _L0_conv_in["b2_offb"],
        "L0_conv_b2_modw": _L0_conv_in["b2_modw"],
        "L0_conv_b2_modb": _L0_conv_in["b2_modb"],
        "L0_conv_b2_regw": _L0_conv_in["b2_regw"],
        "L0_conv_b2_gng": _L0_conv_in["b2_gng"],
        "L0_conv_b2_gnb": _L0_conv_in["b2_gnb"],
        "L0_conv_b3_offw": _L0_conv_in["b3_offw"],
        "L0_conv_b3_offb": _L0_conv_in["b3_offb"],
        "L0_conv_b3_modw": _L0_conv_in["b3_modw"],
        "L0_conv_b3_modb": _L0_conv_in["b3_modb"],
        "L0_conv_b3_regw": _L0_conv_in["b3_regw"],
        "L0_conv_b3_gng": _L0_conv_in["b3_gng"],
        "L0_conv_b3_gnb": _L0_conv_in["b3_gnb"],
        "L0_conv_b4_offw": _L0_conv_in["b4_offw"],
        "L0_conv_b4_offb": _L0_conv_in["b4_offb"],
        "L0_conv_b4_modw": _L0_conv_in["b4_modw"],
        "L0_conv_b4_modb": _L0_conv_in["b4_modb"],
        "L0_conv_b4_regw": _L0_conv_in["b4_regw"],
        "L0_conv_b4_gng": _L0_conv_in["b4_gng"],
        "L0_conv_b4_gnb": _L0_conv_in["b4_gnb"],
        "L0_conv_pool_w": _L0_conv_in["pool_w"],
        "L0_conv_pool_gng": _L0_conv_in["pool_gng"],
        "L0_conv_pool_gnb": _L0_conv_in["pool_gnb"],
        "L0_conv_fuse_w": _L0_conv_in["fuse_w"],
        "L0_conv_fuse_gng": _L0_conv_in["fuse_gng"],
        "L0_conv_fuse_gnb": _L0_conv_in["fuse_gnb"],
        "L0_ffn_router_w": _L0_ffn_in["router_w"],
        "L0_ffn_router_b": _L0_ffn_in["router_b"],
        "L0_ffn_expert_w": _L0_ffn_in["expert_w"],
        "L0_ffn_expert_b": _L0_ffn_in["expert_b"],
        "L1_conv_in_proj_w": _L1_conv_in["in_proj_w"],
        "L1_conv_dwconv_w": _L1_conv_in["dwconv_w"],
        "L1_conv_conv1d_w": _L1_conv_in["conv1d_w"],
        "L1_conv_conv1d_b": _L1_conv_in["conv1d_b"],
        "L1_conv_x_proj_w": _L1_conv_in["x_proj_w"],
        "L1_conv_dt_proj_w": _L1_conv_in["dt_proj_w"],
        "L1_conv_dt_proj_b": _L1_conv_in["dt_proj_b"],
        "L1_conv_A_log": _L1_conv_in["A_log"],
        "L1_conv_D": _L1_conv_in["D"],
        "L1_conv_out_proj_w": _L1_conv_in["out_proj_w"],
        "L1_conv_ca_fc1_w": _L1_conv_in["ca_fc1_w"],
        "L1_conv_ca_fc2_w": _L1_conv_in["ca_fc2_w"],
        "L1_conv_sa_conv_w": _L1_conv_in["sa_conv_w"],
        "L1_ffn_gate_w": _L1_ffn_in["gate_w"],
        "L1_ffn_gate_b": _L1_ffn_in["gate_b"],
        "L1_ffn_weight1": _L1_ffn_in["weight1"],
        "L1_ffn_weight2": _L1_ffn_in["weight2"],
    }

def reference(x, L0_conv_b1_offw, L0_conv_b1_offb, L0_conv_b1_modw, L0_conv_b1_modb, L0_conv_b1_regw, L0_conv_b1_gng, L0_conv_b1_gnb, L0_conv_b2_offw, L0_conv_b2_offb, L0_conv_b2_modw, L0_conv_b2_modb, L0_conv_b2_regw, L0_conv_b2_gng, L0_conv_b2_gnb, L0_conv_b3_offw, L0_conv_b3_offb, L0_conv_b3_modw, L0_conv_b3_modb, L0_conv_b3_regw, L0_conv_b3_gng, L0_conv_b3_gnb, L0_conv_b4_offw, L0_conv_b4_offb, L0_conv_b4_modw, L0_conv_b4_modb, L0_conv_b4_regw, L0_conv_b4_gng, L0_conv_b4_gnb, L0_conv_pool_w, L0_conv_pool_gng, L0_conv_pool_gnb, L0_conv_fuse_w, L0_conv_fuse_gng, L0_conv_fuse_gnb, L0_ffn_router_w, L0_ffn_router_b, L0_ffn_expert_w, L0_ffn_expert_b, L1_conv_in_proj_w, L1_conv_dwconv_w, L1_conv_conv1d_w, L1_conv_conv1d_b, L1_conv_x_proj_w, L1_conv_dt_proj_w, L1_conv_dt_proj_b, L1_conv_A_log, L1_conv_D, L1_conv_out_proj_w, L1_conv_ca_fc1_w, L1_conv_ca_fc2_w, L1_conv_sa_conv_w, L1_ffn_gate_w, L1_ffn_gate_b, L1_ffn_weight1, L1_ffn_weight2):
    import jax
    import jax.numpy as jnp
    def _L0_conv_ref(x, b1_offw, b1_offb, b1_modw, b1_modb, b1_regw, b1_gng, b1_gnb, b2_offw, b2_offb, b2_modw, b2_modb, b2_regw, b2_gng, b2_gnb, b3_offw, b3_offb, b3_modw, b3_modb, b3_regw, b3_gng, b3_gnb, b4_offw, b4_offb, b4_modw, b4_modb, b4_regw, b4_gng, b4_gnb, pool_w, pool_gng, pool_gnb, fuse_w, fuse_gng, fuse_gnb):
        import jax, jax.numpy as jnp
        import numpy as np
        GN_GROUPS = 16
        EPS = 1e-05

        def conv2d(x, w, b=None, padding=0):
            out = jax.lax.conv_general_dilated(x, w, (1, 1), [(padding, padding), (padding, padding)], dimension_numbers=('NCHW', 'OIHW', 'NCHW'))
            if b is not None:
                out = out + b[None, :, None, None]
            return out

        def group_norm(x, gamma, beta):
            B, C, H, W = x.shape
            xg = x.reshape(B, GN_GROUPS, C // GN_GROUPS, H, W)
            m = xg.mean(axis=(2, 3, 4), keepdims=True)
            v = xg.var(axis=(2, 3, 4), keepdims=True)
            xg = (xg - m) * jax.lax.rsqrt(v + EPS)
            return xg.reshape(B, C, H, W) * gamma[None, :, None, None] + beta[None, :, None, None]

        def bilinear_sample(x, py, px):
            B, C, H, W = x.shape
            y0 = jnp.floor(py)
            x0 = jnp.floor(px)
            xf = x.reshape(B, C, H * W)

            def gather(yi, xi):
                valid = (yi >= 0) & (yi <= H - 1) & (xi >= 0) & (xi <= W - 1)
                yc = jnp.clip(yi, 0, H - 1).astype(jnp.int32)
                xc = jnp.clip(xi, 0, W - 1).astype(jnp.int32)
                idx = (yc * W + xc).reshape(B, -1)
                g = jnp.take_along_axis(xf, idx[:, None, :], axis=2)
                g = g.reshape(B, C, *yi.shape[1:])
                return g * valid[:, None].astype(x.dtype)
            wy = (py - y0)[:, None]
            wx = (px - x0)[:, None]
            v00 = gather(y0, x0)
            v01 = gather(y0, x0 + 1)
            v10 = gather(y0 + 1, x0)
            v11 = gather(y0 + 1, x0 + 1)
            return v00 * (1 - wy) * (1 - wx) + v01 * (1 - wy) * wx + v10 * wy * (1 - wx) + v11 * wy * wx

        def deform_conv(x, off_w, off_b, mod_w, mod_b, reg_w, k, pad):
            B, C, H, W = x.shape
            offset = conv2d(x, off_w, off_b, pad)
            mask = 2.0 * jax.nn.sigmoid(conv2d(x, mod_w, mod_b, pad))
            off = offset.reshape(B, k * k, 2, H, W)
            ky, kx = jnp.meshgrid(jnp.arange(k), jnp.arange(k), indexing='ij')
            base_y = (jnp.arange(H) - pad).astype(x.dtype)[None, None, :, None] + ky.reshape(1, -1, 1, 1).astype(x.dtype)
            base_x = (jnp.arange(W) - pad).astype(x.dtype)[None, None, None, :] + kx.reshape(1, -1, 1, 1).astype(x.dtype)
            py = base_y + off[:, :, 0]
            px = base_x + off[:, :, 1]
            sampled = bilinear_sample(x, py, px) * mask[:, None]
            O = reg_w.shape[0]
            return jnp.einsum('bckhw,ock->bohw', sampled, reg_w.reshape(O, C, k * k))

        def branch(x, off_w, off_b, mod_w, mod_b, reg_w, gng, gnb, k, pad):
            y = deform_conv(x, off_w, off_b, mod_w, mod_b, reg_w, k, pad)
            return jax.nn.relu(group_norm(y, gng, gnb))

        def _forward(x, b1_offw, b1_offb, b1_modw, b1_modb, b1_regw, b1_gng, b1_gnb, b2_offw, b2_offb, b2_modw, b2_modb, b2_regw, b2_gng, b2_gnb, b3_offw, b3_offb, b3_modw, b3_modb, b3_regw, b3_gng, b3_gnb, b4_offw, b4_offb, b4_modw, b4_modb, b4_regw, b4_gng, b4_gnb, pool_w, pool_gng, pool_gnb, fuse_w, fuse_gng, fuse_gnb):
            x1 = branch(x, b1_offw, b1_offb, b1_modw, b1_modb, b1_regw, b1_gng, b1_gnb, 1, 0)
            x2 = branch(x, b2_offw, b2_offb, b2_modw, b2_modb, b2_regw, b2_gng, b2_gnb, 1, 0)
            x3 = branch(x, b3_offw, b3_offb, b3_modw, b3_modb, b3_regw, b3_gng, b3_gnb, 3, 1)
            x4 = branch(x, b4_offw, b4_offb, b4_modw, b4_modb, b4_regw, b4_gng, b4_gnb, 7, 3)
            xm = x.mean(axis=(2, 3), keepdims=True)
            x5 = jax.nn.relu(group_norm(conv2d(xm, pool_w), pool_gng, pool_gnb))
            x5 = jnp.broadcast_to(x5, x1.shape)
            cat = jnp.concatenate([x1, x2, x3, x4, x5], axis=1)
            out = jax.nn.relu(group_norm(conv2d(cat, fuse_w), fuse_gng, fuse_gnb))
            return out
        return _forward(x, b1_offw, b1_offb, b1_modw, b1_modb, b1_regw, b1_gng, b1_gnb, b2_offw, b2_offb, b2_modw, b2_modb, b2_regw, b2_gng, b2_gnb, b3_offw, b3_offb, b3_modw, b3_modb, b3_regw, b3_gng, b3_gnb, b4_offw, b4_offb, b4_modw, b4_modb, b4_regw, b4_gng, b4_gnb, pool_w, pool_gng, pool_gnb, fuse_w, fuse_gng, fuse_gnb)

    def _L0_ffn_ref(x, router_w, router_b, expert_w, expert_b):
        import jax, jax.numpy as jnp
        import numpy as np
        B, N, D, C, E, K = (8, 8192, 128, 128, 8, 2)
        router_probs = jax.nn.softmax(x @ router_w + router_b, axis=-1)
        top_p, top_i = jax.lax.top_k(router_probs, K)
        top_p = top_p / jnp.sum(top_p, axis=-1, keepdims=True)
        expert_out = jnp.einsum('bnd,edc->bnec', x, expert_w) + expert_b
        gathered = jnp.take_along_axis(expert_out, top_i[..., None], axis=2)
        return jnp.einsum('bnk,bnkc->bnc', top_p, gathered)

    def _L1_conv_ref(hidden_states, in_proj_w, dwconv_w, conv1d_w, conv1d_b, x_proj_w, dt_proj_w, dt_proj_b, A_log, D, out_proj_w, ca_fc1_w, ca_fc2_w, sa_conv_w):
        import jax, jax.numpy as jnp
        import numpy as np
        from jax import lax
        B, DM, H, W = (2, 128, 64, 64)
        DI = 2 * DM
        DS = 16
        DC = 4
        DTR = 8

        def silu(x):
            return x * jax.nn.sigmoid(x)
        b, dm, h, w = hidden_states.shape
        L = h * w
        xz = jnp.einsum('ed,bdhw->behw', in_proj_w, hidden_states)
        xz = lax.conv_general_dilated(xz, dwconv_w, (1, 1), [(2, 2), (2, 2)], dimension_numbers=('NCHW', 'OIHW', 'NCHW'), feature_group_count=2 * DI)
        xz = xz.reshape(b, 2 * DI, L)
        x, z = (xz[:, :DI], xz[:, DI:])

        def ca_branch(v):
            v = silu(jnp.einsum('rd,bdo->bro', ca_fc1_w, v))
            return jnp.einsum('dr,bro->bdo', ca_fc2_w, v)
        avg = jnp.mean(x, axis=-1, keepdims=True)
        mx = jnp.max(x, axis=-1, keepdims=True)
        x = jax.nn.sigmoid(ca_branch(avg) + ca_branch(mx)) * x
        stats = jnp.concatenate([jnp.mean(z, axis=1, keepdims=True), jnp.max(z, axis=1, keepdims=True)], axis=1)
        att = lax.conv_general_dilated(stats, sa_conv_w, (1,), [(3, 3)], dimension_numbers=('NCH', 'OIH', 'NCH'))
        z = jax.nn.sigmoid(att) * z
        x = lax.conv_general_dilated(x, conv1d_w, (1,), [(DC - 1, 0)], dimension_numbers=('NCH', 'OIH', 'NCH'), feature_group_count=DI)
        x = silu(x + conv1d_b[None, :, None])
        x_dbl = jnp.einsum('ed,bdl->bel', x_proj_w, x)
        dt_lo = x_dbl[:, :DTR]
        Bm = x_dbl[:, DTR:DTR + DS]
        Cm = x_dbl[:, DTR + DS:]
        delta = jnp.einsum('dr,brl->bdl', dt_proj_w, dt_lo)
        delta = jax.nn.softplus(delta + dt_proj_b[None, :, None])
        A = -jnp.exp(A_log)
        dA = jnp.exp(jnp.einsum('bdl,dn->lbdn', delta, A))
        dBu = jnp.einsum('bdl,bnl,bdl->lbdn', delta, Bm, x)
        Ct = jnp.transpose(Cm, (2, 0, 1))

        def step(s, inp):
            a, bu, c = inp
            s = a * s + bu
            return (s, jnp.einsum('bdn,bn->bd', s, c))
        _, ys = lax.scan(step, jnp.zeros((b, DI, DS), x.dtype), (dA, dBu, Ct))
        y = jnp.transpose(ys, (1, 2, 0))
        y = y + x * D[None, :, None]
        y = y * silu(z)
        out = jnp.einsum('md,bdl->blm', out_proj_w, y)
        return jnp.transpose(out, (0, 2, 1)).reshape(b, dm, h, w)

    def _L1_ffn_ref(x, gate_w, gate_b, weight1, weight2):
        import jax, jax.numpy as jnp
        import numpy as np
        B, S, D, E, H, O, K = (512, 2048, 128, 64, 512, 128, 8)
        Bn, Sn, Dn = x.shape
        logits = jnp.einsum('bsd,ed->bse', x, gate_w) + gate_b
        probs = jax.nn.softmax(logits, axis=1)
        vals, idx = jax.lax.top_k(probs.transpose(0, 2, 1), K)
        topv = vals.transpose(0, 2, 1)
        topi = idx.transpose(0, 2, 1)
        flat_idx = topi.reshape(Bn, K * E)
        gathered = jnp.take_along_axis(x, flat_idx[:, :, None], axis=1)
        gathered = gathered.reshape(Bn, K, E, Dn)
        pooled = jnp.einsum('bked,bke->bed', gathered, topv)
        ones = jnp.ones((E, Bn, 1), dtype=x.dtype)
        h = jnp.concatenate([pooled.transpose(1, 0, 2), ones], axis=-1)
        h = jax.nn.gelu(jnp.einsum('ebd,edh->ebh', h, weight1), approximate=False)
        h = jnp.concatenate([h, ones], axis=-1)
        out = jnp.einsum('ebh,eho->ebo', h, weight2)
        out = out.transpose(1, 0, 2)
        weighted = jnp.einsum('beo,bke->bkeo', out, topv).reshape(Bn, K * E, O)
        outputs = jnp.zeros((Bn, Sn, O), dtype=x.dtype)
        outputs = outputs.at[jnp.arange(Bn)[:, None], flat_idx].add(weighted)
        return outputs

    def _gn(v, G=32, eps=1e-5):
        B_, C_, H_, W_ = v.shape
        g = v.reshape(B_, G, C_ // G, H_, W_)
        m = jnp.mean(g, axis=(2, 3, 4), keepdims=True)
        s = jnp.var(g, axis=(2, 3, 4), keepdims=True)
        return ((g - m) / jnp.sqrt(s + eps)).reshape(v.shape)

    def _ln_c(v, eps=1e-6):
        m = jnp.mean(v, axis=1, keepdims=True)
        s = jnp.var(v, axis=1, keepdims=True)
        return (v - m) / jnp.sqrt(s + eps)

    def _ln_t(v, eps=1e-5):
        m = jnp.mean(v, axis=-1, keepdims=True)
        s = jnp.var(v, axis=-1, keepdims=True)
        return (v - m) / jnp.sqrt(s + eps)

    def _to_tokens(v):
        B_, C_, H_, W_ = v.shape
        return v.reshape(B_, C_, H_ * W_).transpose(0, 2, 1)
    def _from_tokens(t, like):
        B_, C_, H_, W_ = like.shape
        return t.transpose(0, 2, 1).reshape(B_, C_, H_, W_)

    x = x + _L0_conv_ref(_ln_c(x), L0_conv_b1_offw, L0_conv_b1_offb, L0_conv_b1_modw, L0_conv_b1_modb, L0_conv_b1_regw, L0_conv_b1_gng, L0_conv_b1_gnb, L0_conv_b2_offw, L0_conv_b2_offb, L0_conv_b2_modw, L0_conv_b2_modb, L0_conv_b2_regw, L0_conv_b2_gng, L0_conv_b2_gnb, L0_conv_b3_offw, L0_conv_b3_offb, L0_conv_b3_modw, L0_conv_b3_modb, L0_conv_b3_regw, L0_conv_b3_gng, L0_conv_b3_gnb, L0_conv_b4_offw, L0_conv_b4_offb, L0_conv_b4_modw, L0_conv_b4_modb, L0_conv_b4_regw, L0_conv_b4_gng, L0_conv_b4_gnb, L0_conv_pool_w, L0_conv_pool_gng, L0_conv_pool_gnb, L0_conv_fuse_w, L0_conv_fuse_gng, L0_conv_fuse_gnb)
    t = _to_tokens(x)
    t = t + _L0_ffn_ref(_ln_t(t), L0_ffn_router_w, L0_ffn_router_b, L0_ffn_expert_w, L0_ffn_expert_b)
    x = _from_tokens(t, x)
    x = x + _L1_conv_ref(_ln_c(x), L1_conv_in_proj_w, L1_conv_dwconv_w, L1_conv_conv1d_w, L1_conv_conv1d_b, L1_conv_x_proj_w, L1_conv_dt_proj_w, L1_conv_dt_proj_b, L1_conv_A_log, L1_conv_D, L1_conv_out_proj_w, L1_conv_ca_fc1_w, L1_conv_ca_fc2_w, L1_conv_sa_conv_w)
    t = _to_tokens(x)
    t = t + _L1_ffn_ref(_ln_t(t), L1_ffn_gate_w, L1_ffn_gate_b, L1_ffn_weight1, L1_ffn_weight2)
    x = _from_tokens(t, x)
    return x


_drawn_inputs = setup_inputs


def setup_inputs(seed=0):
    import zlib

    import numpy as np

    out = dict(_drawn_inputs(seed))
    spreads = {'L0_conv_b1_offb': (0.0, 0.1),
     'L0_conv_b1_gng': (1.0, 0.2),
     'L0_conv_b1_gnb': (0.0, 0.1),
     'L0_conv_b2_offb': (0.0, 0.1),
     'L0_conv_b2_gng': (1.0, 0.2),
     'L0_conv_b2_gnb': (0.0, 0.1),
     'L0_conv_b3_offb': (0.0, 0.1),
     'L0_conv_b3_modb': (0.0, 0.1),
     'L0_conv_b3_gng': (1.0, 0.2),
     'L0_conv_b3_gnb': (0.0, 0.1),
     'L0_conv_b4_offb': (0.0, 0.1),
     'L0_conv_b4_modb': (0.0, 0.1),
     'L0_conv_b4_gng': (1.0, 0.2),
     'L0_conv_b4_gnb': (0.0, 0.1),
     'L0_conv_pool_gng': (1.0, 0.2),
     'L0_conv_pool_gnb': (0.0, 0.1),
     'L0_conv_fuse_gng': (1.0, 0.2),
     'L0_conv_fuse_gnb': (0.0, 0.1),
     'L0_ffn_router_b': (0.0, 0.1),
     'L0_ffn_expert_b': (0.0, 0.1),
     'L1_conv_conv1d_b': (0.0, 0.8),
     'L1_conv_D': (1.0, 0.6),
     'L1_ffn_gate_b': (0.0, 0.1)}
    factors = {'L1_conv_in_proj_w': 8.0,
     'L1_conv_dwconv_w': 8.0,
     'L1_conv_conv1d_w': 8.0,
     'L1_conv_x_proj_w': 8.0,
     'L1_conv_dt_proj_w': 8.0,
     'L1_conv_dt_proj_b': 8.0,
     'L1_conv_A_log': 8.0,
     'L1_conv_out_proj_w': 8.0,
     'L1_conv_ca_fc1_w': 8.0,
     'L1_conv_ca_fc2_w': 8.0,
     'L1_conv_sa_conv_w': 8.0,
     'L1_ffn_gate_w': 8.0,
     'L1_ffn_weight1': 8.0,
     'L1_ffn_weight2': 8.0}
    for name, (base, spread) in spreads.items():
        noise = np.random.default_rng([zlib.crc32(name.encode()), seed]).standard_normal(out[name].shape)
        drawn = base * np.exp(spread * noise) if base else spread * noise
        out[name] = jnp.asarray(drawn.astype(out[name].dtype))
    for name, factor in factors.items():
        out[name] = (out[name] * factor).astype(out[name].dtype)
    return out
```

```python
from contextlib import ExitStack

import numpy as np

import concourse.bass as bass
from concourse import mybir

ALU = mybir.AluOpType
ACT = mybir.ActivationFunctionType
F32 = mybir.dt.float32
I32 = mybir.dt.int32
AX_X = mybir.AxisListType.X

P = 128
B = 2
H = W = 64
L = H * W
N = B * L
TILE = 128
TILES = N // TILE
TPG = 4
GROUPS = TILES // TPG
GPB = GROUPS // B
SPAN = TPG * TILE
O = 256
HALVES = O // P

BRANCHES = [("b4", 7), ("b3", 3), ("b1", 1), ("b2", 1)]
TAPS_OF = [k * k for _, k in BRANCHES]
TAPS = sum(TAPS_OF)
FIRST_TAP = [sum(TAPS_OF[:i]) for i in range(len(BRANCHES))]
KMAX = 7
HALO = KMAX // 2
PADDED = H + 2 * HALO
PATCH_ROWS = 2 + 2 * HALO
COLS = 3 * TAPS
QSIDE = H + 1
QROWS = QSIDE * QSIDE


class Tally:

    def __init__(self, eng, sem, base=0):
        self.eng, self.sem, self.base, self.n = eng, sem, base, 0

    def done(self, ins):
        ins.then_inc(self.sem, 1)
        self.n += 1

    def settle(self):
        self.eng.wait_ge(self.sem, self.base + self.n)


RETIRED = []


def sweep(nc):
    nc.clear_and_free_semaphores(list(RETIRED))
    RETIRED.clear()
    nc.all_engine_barrier()


def tools(nc, ctx, tag):
    held = []
    ctx.callback(lambda: RETIRED.extend(held))

    def sb(name, shape, dt=F32):
        return ctx.enter_context(nc.sbuf_tensor(f"{tag}_{name}", shape, dt))

    def pb(name, shape, dt=F32):
        return ctx.enter_context(nc.psum_tensor(f"{tag}_{name}", shape, dt))

    def sem(name):
        held.append(nc.alloc_semaphore(f"{tag}_{name}"))
        return held[-1]

    return sb, pb, sem


def make_identity(nc, ident):
    with ExitStack() as ctx:
        _, _, sem = tools(nc, ctx, "id")
        filled = sem("filled")
        block = ctx.enter_context(nc.Block())

        @block.gpsimd
        def _(pool):
            nc.gpsimd.memset(ident[:], 0.0).then_inc(filled, 1)
            pool.wait_ge(filled, 1)
            nc.gpsimd.affine_select(out=ident[:], in_=ident[:], compare_op=ALU.not_equal, fill=1.0, base=0,
                                    pattern=[[-1, P]], channel_multiplier=1).then_inc(filled, 1)
            pool.wait_ge(filled, 2)


def clear(nc, tag, tile):
    with ExitStack() as ctx:
        _, _, sem = tools(nc, ctx, tag)
        cleared = sem("cleared")
        block = ctx.enter_context(nc.Block())

        @block.vector
        def _(dve):
            nc.vector.memset(tile[:], 0.0).then_inc(cleared, 1)
            dve.wait_ge(cleared, 1)


def layer_norm(nc, tag, ident, x_dram, tok_sb, eps, chan_at=None):
    with ExitStack() as ctx:
        sb, pb, sem = tools(nc, ctx, tag)
        eps_sb = sb("eps", [P, 1])
        x_in = [sb(f"x_in{s}", [P, SPAN]) for s in range(2)]
        nrm = [sb(f"nrm{s}", [P, TPG, P]) for s in range(2)]
        stats = sb("stats", [P, 2, TPG, 6])
        mv = sb("mv", [P, 2, TPG, 2])
        std = sb("std", [P, 2, TPG])
        rstd = sb("rstd", [P, 2, TPG])
        tok_ps = [pb(f"tok_ps{s}", [P, TPG, TILE]) for s in range(2)]
        chan_ps = [pb(f"chan_ps{s}", [P, SPAN]) for s in range(2)]
        eps_set = sem("eps_set")
        loaded = [sem(f"loaded{s}") for s in range(2)]
        turned = sem("turned")
        tok_free = sem("tok_free")
        counted = sem("counted")
        moments = sem("moments")
        rooted = sem("rooted")
        normed = sem("normed")
        kept = sem("kept")
        back = sem("back")
        chan_free = sem("chan_free")
        steps = sem("steps")
        PER = 3 * TPG + 1
        block = ctx.enter_context(nc.Block())

        @block.sync
        def _(sp):
            for s in range(2):
                sp.dma_start(x_in[s][:], x_dram[0, :, s * SPAN:(s + 1) * SPAN]).then_inc(loaded[s], 16)
            for b in range(B):
                with sp.Fori(0, GPB // 2 - (1 if b == 0 else 0)) as i:
                    for s in range(2):
                        gl = 2 * i + s + (2 if b == 0 else 0)
                        g = b * GPB + gl
                        sp.wait_ge(turned, g - 1)
                        sp.dma_start(x_in[s][:], x_dram[b, :, bass.ds(gl * SPAN, SPAN)]).then_inc(loaded[s], 16)

        @block.tensor
        def _(pe):
            pe.sem_inc(back, 2)

            def turn(g, s):
                pe.wait_ge(loaded[s], (g + 2 - s) * 8)
                pe.wait_ge(tok_free, g + 1)
                for j in range(TPG):
                    last = nc.tensor.transpose(tok_ps[s][:, j, :], x_in[s][:, j * TILE:(j + 1) * TILE], ident[:])
                last.then_inc(turned, 1)

            def turn_back(g, s):
                if chan_at is None:
                    return
                pe.wait_ge(chan_free, g + 1)
                pe.wait_ge(normed, g + 1)
                for j in range(TPG):
                    last = nc.tensor.transpose(chan_ps[s][:, j * TILE:(j + 1) * TILE], nrm[s][:, j, :], ident[:])
                last.then_inc(back, 1)

            turn(0, 0)
            with pe.Fori(0, GROUPS // 2 - 1) as i:
                turn(2 * i + 1, 1)
                turn_back(2 * i, 0)
                turn(2 * i + 2, 0)
                turn_back(2 * i + 1, 1)
            turn(GROUPS - 1, 1)
            turn_back(GROUPS - 2, 0)
            turn_back(GROUPS - 1, 1)

        @block.vector
        def _(dve):
            nc.vector.memset(eps_sb[:], eps).then_inc(eps_set, 1)
            dve.sem_inc(tok_free, 2)
            with dve.Fori(0, GROUPS // 2) as i:
                for s in range(2):
                    g = 2 * i + s
                    own = Tally(dve, steps, g * PER)
                    dve.wait_ge(turned, g + 1)
                    for j in range(TPG):
                        own.done(nc.vector.bn_stats(stats[:, s, j, :], tok_ps[s][:, j, :]))
                    own.settle()
                    dve.sem_inc(counted, 1)
                    for j in range(TPG):
                        own.done(nc.vector.bn_aggr(mv[:, s, j, :], stats[:, s, j, :]))
                    own.settle()
                    dve.sem_inc(moments, 1)
                    dve.wait_ge(rooted, g + 1)
                    own.done(nc.vector.reciprocal(rstd[:, s, :], std[:, s, :]))
                    own.settle()
                    if tok_sb is not None:
                        dve.wait_ge(kept, g + 1)
                    if chan_at is not None:
                        dve.wait_ge(back, g + 1)
                    for j in range(TPG):
                        own.done(nc.vector.tensor_scalar(nrm[s][:, j, :], tok_ps[s][:, j, :], mv[:, s, j, 0:1],
                                                         rstd[:, s, j:j + 1], ALU.subtract, ALU.mult))
                    own.settle()
                    dve.sem_inc(normed, 1)
                    dve.sem_inc(tok_free, 1)
                    assert own.n == PER, own.n

        @block.gpsimd
        def _(pool):
            if tok_sb is None:
                return
            pool.sem_inc(kept, 2)
            with pool.Fori(0, GROUPS // 2) as i:
                for s in range(2):
                    g = 2 * i + s
                    pool.wait_ge(normed, g + 1)
                    nc.gpsimd.tensor_copy(tok_sb[:, bass.ds(g * TPG, TPG), :], nrm[s][:]).then_inc(kept, 1)
            pool.wait_ge(kept, 2 + GROUPS)

        @block.scalar
        def _(act):
            act.wait_ge(eps_set, 1)
            act.sem_inc(chan_free, 2)

            def root(g, s):
                act.wait_ge(moments, g + 1)
                nc.scalar.activation(std[:, s, :], mv[:, s, :, 1], ACT.Sqrt, bias=eps_sb[:]).then_inc(rooted, 1)

            def put_back(b, gl, s):
                if chan_at is None:
                    return
                act.wait_ge(back, b * GPB + gl + 3)
                dest = chan_at(b, gl)
                src = chan_ps[s][:]
                if len(dest.shape) == 3:
                    src = src.rearrange("p (r c) -> p r c", c=dest.shape[2])
                nc.scalar.activation(dest, src, ACT.Copy).then_inc(chan_free, 1)

            for b in range(B):
                g0 = b * GPB
                root(g0, 0)
                with act.Fori(0, GPB // 2 - 1) as i:
                    root(g0 + 2 * i + 1, 1)
                    put_back(b, 2 * i, 0)
                    root(g0 + 2 * i + 2, 0)
                    put_back(b, 2 * i + 1, 1)
                root(g0 + GPB - 1, 1)
                put_back(b, GPB - 2, 0)
                put_back(b, GPB - 1, 1)
            if chan_at is not None:
                act.wait_ge(chan_free, 2 + GROUPS)


def corner_table(nc, tok_sb, table):
    with ExitStack() as ctx:
        sb, _, sem = tools(nc, ctx, "ct")
        zeros = sb("zeros", [QSIDE, 2 * P])
        cleared = sem("cleared")
        written = sem("written")
        count = [0]
        block = ctx.enter_context(nc.Block())
        quads = table.rearrange("(b y x) (v h c) -> b y x v h c", b=B, y=QSIDE, v=2, h=2)

        @block.gpsimd
        def _(pool):
            nc.gpsimd.memset(zeros[:], 0.0).then_inc(cleared, 1)

        @block.sync
        def _(sp):
            def put(dst, src):
                sp.dma_start(dst, src).then_inc(written, 16)
                count[0] += 16

            sp.wait_ge(cleared, 1)
            zrow = zeros[:].rearrange("p (h c) -> p h c", h=2)
            for b in range(B):
                put(quads[b, 0, :, 0], zrow)
                put(quads[b, QSIDE - 1, :, 1], zrow)
            sp.wait_ge(written, count[0])
            for b in range(B):
                put(quads[b, :, 0, :, 0], zrow)
                put(quads[b, :, QSIDE - 1, :, 1], zrow)
            sp.wait_ge(written, count[0])
            for b in range(B):
                for r in range(2):
                    src = tok_sb[r * W:(r + 1) * W, b * (TILES // B):(b + 1) * (TILES // B), :]
                    for v in range(2):
                        for h in range(2):
                            dst = quads[b, 1 + r - v:r - v + H:2, 1 - h:1 - h + W, v, h]
                            put(dst.rearrange("t x c -> x t c"), src)
            sp.wait_ge(written, count[0])


STRIP_ROWS = SPAN // W + 2 * HALO
HALF_ROWS = STRIP_ROWS - SPAN // W // 2


def keep_strips(nc, xpad, strips, mean_sb):
    with ExitStack() as ctx:
        sb, _, sem = tools(nc, ctx, "ks")
        total = sb("total", [P, B])
        summed = sem("summed")
        kept = sem("kept")
        block = ctx.enter_context(nc.Block())

        @block.sync
        def _(sp):
            for c in range(GROUPS + 2):
                b, gl = divmod(min(c, GROUPS - 1), GPB)
                row = gl * (SPAN // W)
                sp.dma_start(strips[c], xpad[:, b, row:row + STRIP_ROWS, :]).then_inc(kept, 16)
            sp.wait_ge(kept, 16 * (GROUPS + 2))

        @block.vector
        def _(dve):
            for b in range(B):
                nc.vector.tensor_reduce(total[:, b:b + 1], xpad[:, b, HALO:HALO + H, HALO:HALO + W],
                                        mybir.AxisListType.XY, ALU.add).then_inc(summed, 1)
            dve.wait_ge(summed, B)
            nc.vector.tensor_scalar(mean_sb[:], total[:], 1.0 / L, None, ALU.mult).then_inc(summed, 1)
            dve.wait_ge(summed, B + 1)


SLOTS = 4


def deformable(nc, ident, table, strips, offset_w, offset_b, base_pos, row_base, tap_w, y_dram, stats_sb):
    assert TAPS % SLOTS == 0
    UPS = TAPS // SLOTS
    LOOPS = {1: 5, 1 + 6 * SLOTS: 5}
    SORT_AT = (5 * SLOTS, 11 * SLOTS)
    STAGE_AT = {1: 5 * SLOTS + 1, 0: 52}
    COUNT_LATE_AT = {5 * SLOTS + br: br for br in range(1, len(BRANCHES))}
    POSITION_AT, INDEX_AT, COUNT_AT, FACTOR_AT, WEIGHT_AT = 47, 49, 51, 53, 56
    SORTS = 3
    CLEARS = 4 + len(BRANCHES) - 1
    OFFSET_LOADS = 9
    LAST_TAP = [t0 + taps - 1 for t0, taps in zip(FIRST_TAP, TAPS_OF)]
    VT = TPG - 1
    with ExitStack() as ctx:
        sb, pb, sem = tools(nc, ctx, "df")
        w_sb = sb("w", [P, TAPS, O])
        corners = [sb(f"corners{s}", [P, TPG, 4, P]) for s in range(SLOTS)]
        rows = [sb(f"rows{s}", [P, TPG], I32) for s in range(SLOTS)]
        pairs = sb("pairs", [P, TPG, 2, P])
        sampled = [sb(f"sampled{s}", [P, TPG, P]) for s in range(2)]
        turned_sb = [sb(f"turned{s}", [P, SPAN]) for s in range(2)]
        tapw = [sb(f"tapw{s}", [P, O]) for s in range(2)]
        index_sb = sb("index", [P, 2, TAPS, TPG], I32)
        weight_sb = sb("weight", [P, 2, TAPS, TPG, 4])
        ow_sb = sb("ow", [P, KMAX, KMAX, COLS])
        bias_sb = sb("bias", [1, COLS])
        ones = sb("ones", [1, P])
        base_sb = sb("base", [P, 2, TAPS])
        row_sb = sb("row", [P, TILES + TPG])
        first_sb = sb("first", [P, GROUPS + 1])
        strip = sb("strip", [P, STRIP_ROWS, PADDED])
        patch = sb("patch", [P, KMAX, HALF_ROWS * W])
        raw = sb("raw", [P, TPG, 3, TAPS])
        pos = sb("pos", [P, TPG, 2, TAPS])
        flo = sb("flo", [P, TPG, 2, TAPS])
        flo_i = sb("flo_i", [P, TPG, 2, TAPS], I32)
        frac = sb("frac", [P, TPG, 2, TAPS])
        rowi = sb("rowi", [P, TPG, TAPS])
        m_lo = sb("m_lo", [P, TPG, TAPS])
        m_hi = sb("m_hi", [P, TPG, TAPS])
        y_sb = [sb(f"y{br}", [P, HALVES, SPAN]) for br in range(len(BRANCHES))]
        turn_ps = [pb(f"turn_ps{s}", [P, SPAN]) for s in range(2)]
        acc_ps = [pb(f"acc_ps{s}", [P, HALVES, SPAN]) for s in range(2)]
        conv_ps = [pb(f"conv_ps{s}", [P, 512]) for s in range(2)]
        cleared = sem("cleared")
        loaded = sem("loaded")
        strip_loaded = sem("strip_loaded")
        strip_free = sem("strip_free")
        patched = sem("patched")
        convolved = sem("convolved")
        sorted_out = sem("sorted_out")
        offset_ready = sem("offset_ready")
        raw_free = sem("raw_free")
        index_ready = sem("index_ready")
        weight_ready = sem("weight_ready")
        steps = sem("steps")
        w_loaded = sem("w_loaded")
        listed = sem("listed")
        fetch = sem("fetch")
        gathered = [sem(f"gathered{s}") for s in range(SLOTS)]
        slot_free = sem("slot_free")
        weighed_v = sem("weighed_v")
        weighed_a = sem("weighed_a")
        paired = sem("paired")
        summed = sem("summed")
        summed_free = sem("summed_free")
        turned = sem("turned")
        operand = sem("operand")
        multiplied = sem("multiplied")
        section = sem("section")
        acc_free = sem("acc_free")
        y_counted = sem("y_counted")
        y_free = sem("y_free")
        stored = [sem(f"stored{br}") for br in range(len(BRANCHES))]
        block = ctx.enter_context(nc.Block())
        c3, c1 = 3 * TAPS_OF[0], 3 * (TAPS_OF[0] + TAPS_OF[1])
        conv_taps = sorted(((ky, kx) for ky in range(KMAX) for kx in range(KMAX)), key=lambda t: t == (HALO, HALO))

        def group_loop(eng, unit, after=lambda g, ring, tap: None):
            with eng.Fori(0, GROUPS // 2) as q:
                with eng.Fori(0, 2) as ring:
                    g = 2 * q + ring
                    tap = 0
                    while tap < TAPS:
                        rounds = LOOPS.get(tap, 0)
                        if rounds:
                            with eng.Fori(0, rounds) as i:
                                for j in range(SLOTS):
                                    u = tap + j
                                    unit(g, ring, g * UPS + i + u // SLOTS, i * SLOTS + u, u % SLOTS, u % 2)
                        else:
                            unit(g, ring, g * UPS + tap // SLOTS, tap, tap % SLOTS, tap % 2)
                        tap += max(1, rounds * SLOTS)
                        after(g, ring, tap - 1)


        @block.sync
        def _(sp):
            w4, w3, w1, w2 = offset_w
            sp.dma_start(ow_sb[:, :, :, 0:c3], w4).then_inc(loaded, 16)
            for ky in range(3):
                sp.dma_start(ow_sb[:, 2 + ky, 2:5, c3:c1], w3[:, ky]).then_inc(loaded, 16)
            sp.dma_start(ow_sb[:, 3, 3, c1:c1 + 3], w1).then_inc(loaded, 16)
            sp.dma_start(ow_sb[:, 3, 3, c1 + 3:c1 + 6], w2).then_inc(loaded, 16)
            sp.dma_start(bias_sb[:], offset_b).then_inc(loaded, 16)
            sp.dma_start(base_sb[:], base_pos).then_inc(loaded, 16)
            sp.dma_start(row_sb[:, 0:TILES], row_base).then_inc(loaded, 16)
            sp.dma_start(strip[:], strips[0]).then_inc(strip_loaded, 16)
            sp.dma_start(w_sb[:], tap_w).then_inc(w_loaded, 16)
            sp.wait_ge(strip_free, 1)
            sp.dma_start(strip[:], strips[1]).then_inc(strip_loaded, 16)
            sp.sem_inc(y_free, len(BRANCHES))
            with sp.Fori(0, GROUPS // GPB) as b:
                with sp.Fori(0, GPB) as gl:
                    sp.wait_ge(strip_free, b * GPB + gl + 2)
                    sp.dma_start(strip[:], strips[bass.ds(b * GPB + gl + 2, 1)].rearrange("o p r c -> (o p) r c"))\
                        .then_inc(strip_loaded, 16)
                    for br in range(len(BRANCHES)):
                        done = (b * GPB + gl) * len(BRANCHES) + br
                        sp.wait_ge(acc_free, done + 4)
                        for h in range(HALVES):
                            sp.dma_start(y_dram[br][bass.ds(b, 1), h, :, bass.ds(gl * SPAN, SPAN)]
                                         .rearrange("o p n -> (o p) n"), y_sb[br][:, h, :]).then_inc(stored[br], 16)
                        sp.wait_ge(stored[br], (b * GPB + gl + 1) * (16 * HALVES))
                        sp.sem_inc(y_free, 1)

        @block.gpsimd
        def _(pool):
            pool.sem_inc(slot_free, SLOTS)

            def unit(g, ring, use, tap, slot, pair):
                n = g * TAPS + tap
                pool.wait_ge(slot_free, n + 1)
                pool.wait_ge(listed, n + 1)
                pool.sem_inc(fetch, 1)
                for j in range(TPG):
                    nc.gpsimd.indirect_dma_start(
                        corners[slot][:, j].rearrange("p v c -> p (v c)"), None, table,
                        bass.IndirectOffsetOnAxis(ap=rows[slot][:, j:j + 1], axis=0)).then_inc(gathered[slot], 16)

            group_loop(pool, unit)

        @block.vector
        def _(dve):
            def unit(g, ring, use, tap, slot, pair):
                n = g * TAPS + tap
                dve.wait_ge(gathered[slot], (use + 1) * (16 * TPG))
                w = weight_sb[:, bass.ds(ring, 1), bass.ds(tap, 1), 0:VT, :].rearrange("p g k j c -> p (g k j c)")
                view = corners[slot][:, 0:VT].rearrange("p j v c -> p (j v) c")
                nc.vector.tensor_tensor(view, view, w.unsqueeze(2).broadcast_to([P, VT * 4, P]),
                                        ALU.mult).then_inc(weighed_v, 1)
                dve.wait_ge(weighed_v, n + 1)
                dve.wait_ge(weighed_a, 4 * (n + 1))
                dve.wait_ge(summed, n + 1)
                nc.vector.tensor_tensor(pairs[:].rearrange("p j h c -> p j (h c)"),
                                        corners[slot][:, :, 0:2].rearrange("p j h c -> p j (h c)"),
                                        corners[slot][:, :, 2:4].rearrange("p j h c -> p j (h c)"),
                                        ALU.add).then_inc(paired, 1)
                dve.wait_ge(paired, n + 1)
                dve.sem_inc(slot_free, 1)
                dve.wait_ge(turned, n + 1)
                nc.vector.tensor_tensor(sampled[pair][:], pairs[:, :, 0, :], pairs[:, :, 1, :],
                                        ALU.add).then_inc(summed, 1)

            def count(g, br):
                done = g * len(BRANCHES) + br
                dve.wait_ge(acc_free, done + 4)
                for h in range(HALVES):
                    nc.vector.bn_stats(stats_sb[:, br, h, bass.ds((g + 1) * 6, 6)],
                                       y_sb[br][:, h, :]).then_inc(y_counted, 1)

            def positions(c):
                own = Tally(dve, steps, c * PER)
                v = nc.vector

                def wide(ap):
                    return ap.unsqueeze(1).broadcast_to([P, TPG, TAPS])

                rows_of = row_sb[:, bass.ds(c * TPG, TPG)].unsqueeze(2).broadcast_to([P, TPG, TAPS])
                own.done(v.tensor_tensor(pos[:, :, 0, :], wide(base_sb[:, 0, :]), rows_of, ALU.add))
                own.settle()
                dve.wait_ge(offset_ready, c + 1)
                own.done(v.tensor_tensor(pos[:, :, 0, :], pos[:, :, 0, :], raw[:, :, 0, :], ALU.add))
                own.done(v.tensor_tensor(pos[:, :, 1, :], wide(base_sb[:, 1, :]), raw[:, :, 1, :], ALU.add))
                own.settle()
                own.done(v.tensor_scalar(pos[:], pos[:], -1.0, float(H), ALU.max, ALU.min))
                own.settle()
                own.done(v.tensor_copy(flo_i[:], pos[:]))
                own.settle()
                own.done(v.tensor_copy(flo[:], flo_i[:]))
                own.settle()
                assert own.n == PER_POSITION, own.n

            def indices(c, ring):
                own = Tally(dve, steps, c * PER + PER_POSITION)
                v = nc.vector
                first_of = first_sb[:, bass.ds(c, 1)].unsqueeze(2).broadcast_to([P, TPG, TAPS])
                own.done(v.tensor_tensor(frac[:], flo[:], pos[:], ALU.is_gt))
                own.settle()
                own.done(v.tensor_tensor(flo[:], flo[:], frac[:], ALU.subtract))
                own.settle()
                own.done(v.tensor_scalar(flo[:], flo[:], float(H - 1), None, ALU.min))
                own.settle()
                own.done(v.tensor_scalar(rowi[:], flo[:, :, 0, :], float(QSIDE), None, ALU.mult))
                own.settle()
                own.done(v.tensor_tensor(rowi[:], rowi[:], flo[:, :, 1, :], ALU.add))
                own.settle()
                v.tensor_tensor(index_sb[:, bass.ds(ring, 1)].rearrange("p o k j -> p (o j) k"),
                                rowi[:], first_of, ALU.add).then_inc(index_ready, 1)

            def factors(c):
                own = Tally(dve, steps, c * PER + PER_POSITION + PER_INDEX)
                v = nc.vector
                own.done(v.tensor_tensor(frac[:], pos[:], flo[:], ALU.subtract))
                own.settle()
                own.done(v.tensor_scalar(pos[:], frac[:], -1.0, 1.0, ALU.mult, ALU.add))
                own.done(v.scalar_tensor_tensor(out=m_hi[:], in0=raw[:, :, 2, :], scalar=2.0,
                                                in1=frac[:, :, 0, :], op0=ALU.mult, op1=ALU.mult))
                own.settle()
                own.done(v.scalar_tensor_tensor(out=m_lo[:], in0=raw[:, :, 2, :], scalar=2.0,
                                                in1=pos[:, :, 0, :], op0=ALU.mult, op1=ALU.mult))
                own.settle()
                assert own.n == PER_FACTOR, own.n
                dve.sem_inc(raw_free, 1)

            def weights(c, ring):
                own = Tally(dve, steps, c * PER + PER_POSITION + PER_INDEX + PER_FACTOR)
                v = nc.vector
                for k, (m, f) in enumerate(((m_lo, pos), (m_lo, frac), (m_hi, pos), (m_hi, frac))):
                    dst = weight_sb[:, bass.ds(ring, 1), :, :, k].rearrange("p o k j -> p (o j) k")
                    own.done(v.tensor_tensor(dst, m[:], f[:, :, 1, :], ALU.mult))
                own.settle()
                assert own.n == 4, own.n
                dve.sem_inc(weight_ready, 1)

            def after(g, ring, tap):
                if tap in COUNT_LATE_AT:
                    count(g - 1, COUNT_LATE_AT[tap])
                if tap == POSITION_AT:
                    positions(g + 1)
                if tap == INDEX_AT:
                    indices(g + 1, 1 - ring)
                if tap == COUNT_AT:
                    count(g, 0)
                if tap == FACTOR_AT:
                    factors(g + 1)
                if tap == WEIGHT_AT:
                    weights(g + 1, 1 - ring)

            PER_POSITION, PER_INDEX, PER_FACTOR = 6, 5, 4
            PER = PER_POSITION + PER_INDEX + PER_FACTOR + 4
            nc.vector.memset(ones[:], 1.0).then_inc(cleared, 1)
            nc.vector.memset(row_sb[:, TILES:], 0.0).then_inc(cleared, 1)
            nc.vector.memset(first_sb[:, 0:GPB], float(QSIDE + 1)).then_inc(cleared, 1)
            nc.vector.memset(first_sb[:, GPB:], float(QSIDE + 1 + QROWS)).then_inc(cleared, 1)
            for br in range(1, len(BRANCHES)):
                nc.vector.memset(y_sb[br][:], 0.0).then_inc(cleared, 1)
            dve.wait_ge(cleared, CLEARS)
            dve.wait_ge(loaded, 16 * OFFSET_LOADS)
            positions(0)
            indices(0, 0)
            factors(0)
            weights(0, 0)
            dve.sem_inc(summed, 1)
            dve.sem_inc(y_counted, 1)
            group_loop(dve, unit, after)
            for late in range(1, len(BRANCHES)):
                count(GROUPS - 1, late)
            dve.wait_ge(y_counted, HALVES * ((GROUPS + 1) * len(BRANCHES) - 1) + 1)

        @block.tensor
        def _(pe):
            pe.sem_inc(turned, 2)
            pe.sem_inc(multiplied, 2)

            def convolve(c, tile, part, parts):
                s, done = tile % 2, c * TPG + tile
                share = -(-len(conv_taps) // parts)
                if part == 0:
                    if tile % 2 == 0:
                        pe.wait_ge(patched, KMAX * (2 * c + tile // 2 + 1))
                    if not isinstance(done, int) or done >= 2:
                        pe.wait_ge(sorted_out, (done - 1) * SORTS)
                    nc.tensor.matmul(conv_ps[s][:, 0:COLS], ones[:], bias_sb[:], start=True, stop=False)
                for ky, kx in conv_taps[part * share:(part + 1) * share]:
                    middle = (ky, kx) == (HALO, HALO)
                    inner = 2 <= ky <= 4 and 2 <= kx <= 4
                    n = COLS if middle else c1 if inner else c3
                    row = ky + 2 * (tile % 2)
                    m = nc.tensor.matmul(conv_ps[s][:, 0:n], patch[:, kx, row * W:(row + 2) * W],
                                         ow_sb[:, ky, kx, 0:n], start=False, stop=middle,
                                         skip_group_check=not middle)
                    if middle:
                        m.then_inc(convolved, 1)

            def unit(g, tap):
                n, pair = g * TAPS + tap, tap % 2
                br = max(i for i, t0 in enumerate(FIRST_TAP) if t0 <= tap)
                first, last = tap == FIRST_TAP[br], tap == LAST_TAP[br]
                pe.wait_ge(summed, n + 2)
                for j in range(TPG):
                    t = nc.tensor.transpose(turn_ps[pair][:, j * TILE:(j + 1) * TILE], sampled[pair][:, j, :],
                                            ident[:])
                t.then_inc(turned, 1)
                if tap in share_of:
                    convolve(g + 1, *share_of[tap])
                pe.wait_ge(operand, 2 * (n + 1))
                if first:
                    pe.wait_ge(acc_free, g * len(BRANCHES) + br + 2)
                for h in range(HALVES):
                    m = nc.tensor.matmul(acc_ps[br % 2][:, h, :], tapw[pair][:, h * P:(h + 1) * P],
                                         turned_sb[pair][:], start=first, stop=last)
                m.then_inc(multiplied, 1)
                if last:
                    pe.wait_ge(multiplied, n + 3)
                    pe.sem_inc(section, 1)

            share_of = {}
            for tile, (start, parts) in enumerate(((0, 9), (9, 9), (25, 9), (34, 9))):
                share_of.update({start + part: (tile, part, parts) for part in range(parts)})

            pe.wait_ge(cleared, CLEARS)
            pe.wait_ge(loaded, 16 * OFFSET_LOADS)
            for tile in range(TPG):
                convolve(0, tile, 0, 1)
            with pe.Fori(0, GROUPS) as g:
                for tap in range(TAPS):
                    unit(g, tap)

        @block.scalar
        def _(act):
            act.wait_ge(cleared, CLEARS)
            act.sem_inc(acc_free, 3)

            def list_rows(ring, tap, slot):
                nc.scalar.activation(rows[slot][:].unsqueeze(1),
                                     index_sb[:, bass.ds(ring, 1), bass.ds(tap, 1), :].rearrange("p o k j -> p (o k) j"),
                                     ACT.Copy).then_inc(listed, 1)

            def stage(c, half, shifts=range(KMAX)):
                if shifts[0] == 0:
                    act.wait_ge(strip_loaded, 16 * (c + 1))
                row = half * (STRIP_ROWS - HALF_ROWS)
                for kx in shifts:
                    nc.scalar.activation(patch[:, kx].rearrange("p (r c) -> p r c", c=W),
                                         strip[:, row:row + HALF_ROWS, kx:kx + W], ACT.Copy).then_inc(patched, 1)
                if half == 1 and shifts[-1] == KMAX - 1:
                    act.wait_ge(patched, 2 * KMAX * (c + 1))
                    act.sem_inc(strip_free, 1)

            def sort(c, half):
                k4, k3 = TAPS_OF[0], TAPS_OF[1]
                if half == 0 and not isinstance(c, int):
                    act.wait_ge(raw_free, c)
                for j in (2 * half, 2 * half + 1):
                    act.wait_ge(convolved, c * TPG + j + 1)
                    src, dst = conv_ps[j % 2], raw[:, j]
                    nc.scalar.activation(dst[:, :, 0:k4], src[:, 0:c3].rearrange("p (a k) -> p a k", a=3),
                                         ACT.Copy).then_inc(sorted_out, 1)
                    nc.scalar.activation(dst[:, :, k4:k4 + k3], src[:, c3:c1].rearrange("p (a k) -> p a k", a=3),
                                         ACT.Copy).then_inc(sorted_out, 1)
                    nc.scalar.activation(dst[:, :, TAPS - 2:TAPS], src[:, c1:c1 + 6].rearrange("p (k a) -> p a k", k=2),
                                         ACT.Copy).then_inc(sorted_out, 1)
                if half == 1:
                    act.wait_ge(sorted_out, SORTS * TPG * (c + 1))
                    m = raw[:, :, 2, :]
                    nc.scalar.activation(m, m, ACT.Sigmoid).then_inc(offset_ready, 1)

            def weigh(g, ring, use, tap, slot):
                if isinstance(tap, int) and tap == 0:
                    act.wait_ge(weight_ready, g + 1)
                act.wait_ge(gathered[slot], (use + 1) * (16 * TPG))
                if not isinstance(tap, int) or tap + SLOTS < TAPS:
                    list_rows(ring, tap + SLOTS, slot)
                else:
                    act.wait_ge(index_ready, g + 2)
                    list_rows(1 - ring, tap + SLOTS - TAPS, slot)
                for c in range(4):
                    part = corners[slot][:, VT, c, :]
                    w = weight_sb[:, bass.ds(ring, 1), bass.ds(tap, 1), VT, c:c + 1].rearrange("p g k c -> p (g k c)")
                    nc.scalar.activation(part, part, ACT.Copy, scale=w).then_inc(weighed_a, 1)

            def operands(g, tap, pair):
                n = g * TAPS + tap
                act.wait_ge(multiplied, n + 1)
                nc.scalar.activation(tapw[pair][:].unsqueeze(1), w_sb[:, bass.ds(tap, 1), :],
                                     ACT.Copy).then_inc(operand, 1)
                act.wait_ge(turned, n + 3)
                nc.scalar.activation(turned_sb[pair][:], turn_ps[pair][:], ACT.Copy).then_inc(operand, 1)

            def copy_out(g, br):
                done = g * len(BRANCHES) + br
                act.wait_ge(section, done + 1)
                act.wait_ge(y_free, done + 1)
                act.wait_ge(y_counted, counted_before(g, br))
                nc.scalar.activation(y_sb[br][:], acc_ps[br % 2][:], ACT.Copy).then_inc(acc_free, 1)

            def counted_before(g, br):
                return HALVES * (g * len(BRANCHES) + br) + 1

            def unit(g, ring, use, tap, slot, pair):
                weigh(g, ring, use, tap, slot)
                if isinstance(tap, int) and tap == 0:
                    return
                if isinstance(tap, int) and tap - 2 in LAST_TAP:
                    copy_out(g, LAST_TAP.index(tap - 2))
                operands(g, tap - 1, 1 - pair)

            def after(g, ring, tap):
                if tap == SORT_AT[0]:
                    sort(g + 1, 0)
                if tap == SORT_AT[1]:
                    sort(g + 1, 1)
                for half, c in ((1, g + 1), (0, g + 2)):
                    shift = 2 * (tap - STAGE_AT[half])
                    if 0 <= shift < KMAX:
                        stage(c, half, range(shift, min(shift + 2, KMAX)))
                if tap == TAPS - 1:
                    copy_out(g, len(BRANCHES) - 2)
                    operands(g, TAPS - 1, (TAPS - 1) % 2)
                    copy_out(g, len(BRANCHES) - 1)

            stage(0, 0)
            sort(0, 0)
            stage(0, 1)
            sort(0, 1)
            act.wait_ge(index_ready, 1)
            for slot in range(SLOTS):
                list_rows(0, slot, slot)
            stage(1, 0)
            act.wait_ge(w_loaded, 16)
            group_loop(act, unit, after)


EPS_GN = 1e-5
SLOTS_IN = len(BRANCHES) + 1
COLS_GN = B * SLOTS_IN * HALVES


def group_moments(nc, tag, average, mean, var, gamma, beta, scale, shift, cols, eps):
    with ExitStack() as ctx:
        sb, pb, sem = tools(nc, ctx, tag)
        eps_sb = sb("eps", [P, 1])
        gmean = sb("gmean", [P, cols])
        gvar = sb("gvar", [P, cols])
        apart = sb("apart", [P, cols])
        std = sb("std", [P, cols])
        rstd = sb("rstd", [P, cols])
        ps = [pb(f"ps{i}", [P, 512]) for i in range(3)]
        averaged = sem("averaged")
        steps = sem("steps")
        rooted = sem("rooted")
        squared = sem("squared")
        spread = sem("spread")
        block = ctx.enter_context(nc.Block())

        @block.tensor
        def _(pe):
            nc.tensor.matmul(ps[0][:, 0:cols], average[:], mean[:], start=True, stop=True).then_inc(averaged, 1)
            nc.tensor.matmul(ps[1][:, 0:cols], average[:], var[:], start=True, stop=True).then_inc(averaged, 1)
            pe.wait_ge(squared, 1)
            nc.tensor.matmul(ps[2][:, 0:cols], average[:], apart[:], start=True, stop=True).then_inc(averaged, 1)

        @block.scalar
        def _(act):
            act.wait_ge(spread, 1)
            nc.scalar.activation(std[:], gvar[:], ACT.Sqrt, bias=eps_sb[:]).then_inc(rooted, 1)

        @block.vector
        def _(dve):
            own = Tally(dve, steps)
            own.done(nc.vector.memset(eps_sb[:], eps))
            dve.wait_ge(averaged, 2)
            own.done(nc.vector.tensor_copy(gmean[:], ps[0][:, 0:cols]))
            own.settle()
            own.done(nc.vector.tensor_tensor(apart[:], mean[:], gmean[:], ALU.subtract))
            own.settle()
            nc.vector.tensor_tensor(apart[:], apart[:], apart[:], ALU.mult).then_inc(squared, 1)
            own.done(nc.vector.tensor_copy(gvar[:], ps[1][:, 0:cols]))
            own.settle()
            dve.wait_ge(averaged, 3)
            nc.vector.tensor_tensor(gvar[:], gvar[:], ps[2][:, 0:cols], ALU.add).then_inc(spread, 1)
            dve.wait_ge(rooted, 1)
            own.done(nc.vector.reciprocal(rstd[:], std[:]))
            own.settle()
            own.done(nc.vector.tensor_tensor(scale[:], rstd[:], gamma[:], ALU.mult))
            own.settle()
            own.done(nc.vector.tensor_tensor(apart[:], gmean[:], scale[:], ALU.mult))
            own.settle()
            own.done(nc.vector.tensor_tensor(shift[:], beta[:], apart[:], ALU.subtract))
            own.settle()


def fuse(nc, d, y_dram, stats_sb, mean_sb, x_dram, out_dram):
    with ExitStack() as ctx:
        sb, pb, sem = tools(nc, ctx, "fu")
        average = sb("average", [P, P])
        average_f = sb("average_f", [P, P])
        pool_w = sb("pool_w", [P, O])
        fuse_w = sb("fuse_w", [P, SLOTS_IN * HALVES, P])
        gamma = sb("gamma", [P, COLS_GN])
        beta = sb("beta", [P, COLS_GN])
        gamma_f = sb("gamma_f", [P, B])
        beta_f = sb("beta_f", [P, B])
        mean = sb("mean", [P, COLS_GN])
        var = sb("var", [P, COLS_GN])
        scale = sb("scale", [P, COLS_GN])
        shift = sb("shift", [P, COLS_GN])
        scale_f = sb("scale_f", [P, B])
        shift_f = sb("shift_f", [P, B])
        mean_f = sb("mean_f", [P, B])
        var_f = sb("var_f", [P, B])
        fused = sb("fused", [P, N])
        stats_f = sb("stats_f", [P, GROUPS, 6])
        mv = sb("mv", [P, 2])
        pooled = sb("pooled", [P, B * HALVES])
        pooled_part = sb("pooled_part", [P, B])

        def column(b, slot, h):
            return (b * SLOTS_IN + slot) * HALVES + h

        with ExitStack() as c2:
            sb2, pb2, sem2 = tools(nc, c2, "f1")
            mvs = sb2("mvs", [P, B * len(BRANCHES) * HALVES, 2])
            ps = pb2("ps", [P, 512])
            loaded = sem2("loaded")
            steps = sem2("steps")
            product = sem2("product")
            block = c2.enter_context(nc.Block())

            @block.sync
            def _(sp):
                for dst, src in ((average, "average16"), (average_f, "average8"), (pool_w, "pool_w"),
                                 (fuse_w, "fuse_w"), (gamma, "gn_gamma"), (beta, "gn_beta"),
                                 (gamma_f, "fuse_gamma"), (beta_f, "fuse_beta")):
                    sp.dma_start(dst[:], d[src]).then_inc(loaded, 16)
                sp.wait_ge(loaded, 16 * 8)

            @block.tensor
            def _(pe):
                pe.wait_ge(loaded, 16 * 8)
                for h in range(HALVES):
                    nc.tensor.matmul(ps[:, h * B:(h + 1) * B], pool_w[:, h * P:(h + 1) * P], mean_sb[:],
                                     start=True, stop=True).then_inc(product, 1)

            @block.vector
            def _(dve):
                own = Tally(dve, steps)
                own.done(nc.vector.memset(var[:], 0.0))
                cols = [(b, br, h) for b in range(B) for br in range(len(BRANCHES)) for h in range(HALVES)]
                for n, (b, br, h) in enumerate(cols):
                    own.done(nc.vector.bn_aggr(mvs[:, n, :], stats_sb[:, br, h, (1 + b * GPB) * 6:(1 + (b + 1) * GPB) * 6]))
                own.settle()
                for n, (b, br, h) in enumerate(cols):
                    c = column(b, br, h)
                    own.done(nc.vector.tensor_copy(mean[:, c:c + 1], mvs[:, n, 0:1]))
                    own.done(nc.vector.tensor_copy(var[:, c:c + 1], mvs[:, n, 1:2]))
                dve.wait_ge(product, HALVES)
                for b in range(B):
                    for h in range(HALVES):
                        c = column(b, SLOTS_IN - 1, h)
                        own.done(nc.vector.tensor_copy(mean[:, c:c + 1], ps[:, h * B + b:h * B + b + 1]))
                own.settle()

        group_moments(nc, "gm", average, mean, var, gamma, beta, scale, shift, COLS_GN, EPS_GN)

        TERMS = len(BRANCHES) * HALVES
        with ExitStack() as c2:
            sb2, pb2, sem2 = tools(nc, c2, "f2")
            y_in = [[sb2(f"y_in{s}_{t}", [P, SPAN]) for t in range(TERMS)] for s in range(2)]
            part_ps = pb2("part_ps", [P, 512])
            fuse_ps = [pb2(f"fuse_ps{s}", [P, SPAN]) for s in range(2)]
            pool_ready = sem2("pool_ready")
            part = sem2("part")
            part_kept = sem2("part_kept")
            loaded = [sem2(f"loaded{s}") for s in range(2)]
            active = sem2("active")
            multiplied = sem2("multiplied")
            fused_done = sem2("fused_done")
            counted = sem2("counted")
            block = c2.enter_context(nc.Block())

            @block.sync
            def _(sp):
                sp.sem_inc(multiplied, 2)
                for b in range(B):
                    with sp.Fori(0, GPB // 2) as i:
                        for s in range(2):
                            gl = 2 * i + s
                            g = b * GPB + gl
                            sp.wait_ge(multiplied, g + 1)
                            for t in range(TERMS):
                                br, h = t // HALVES, t % HALVES
                                sp.dma_start(y_in[s][t][:], y_dram[br][b, h, :, bass.ds(gl * SPAN, SPAN)])\
                                    .then_inc(loaded[s], 16)

            @block.scalar
            def _(act):
                for b in range(B):
                    for h in range(HALVES):
                        c, n = column(b, SLOTS_IN - 1, h), b * HALVES + h
                        nc.scalar.activation(pooled[:, n:n + 1], mean[:, c:c + 1], ACT.Relu, bias=shift[:, c:c + 1],
                                             scale=scale[:, c:c + 1]).then_inc(pool_ready, 1)
                act.wait_ge(part, 1)
                nc.scalar.activation(pooled_part[:], part_ps[:, 0:B], ACT.Copy).then_inc(part_kept, 1)
                act.wait_ge(part_kept, 1)
                act.sem_inc(fused_done, 2)
                for b in range(B):
                    with act.Fori(0, GPB // 2) as i:
                        for s in range(2):
                            gl = 2 * i + s
                            g = b * GPB + gl
                            act.wait_ge(loaded[s], (b * (GPB // 2) + i + 1) * (16 * TERMS))
                            for t in range(TERMS):
                                c = column(b, t // HALVES, t % HALVES)
                                nc.scalar.activation(y_in[s][t][:], y_in[s][t][:], ACT.Relu,
                                                     bias=shift[:, c:c + 1], scale=scale[:, c:c + 1])\
                                    .then_inc(active, 1)
                            act.wait_ge(multiplied, g + 3)
                            nc.scalar.activation(fused[:, bass.ds(g * SPAN, SPAN)], fuse_ps[s][:], ACT.Identity,
                                                 bias=pooled_part[:, b:b + 1]).then_inc(fused_done, 1)

            @block.tensor
            def _(pe):
                pe.wait_ge(pool_ready, B * HALVES)
                for h in range(HALVES):
                    m = nc.tensor.matmul(part_ps[:, 0:B], fuse_w[:, TERMS + h, :], pooled[:, h:B * HALVES:HALVES],
                                         start=(h == 0), stop=(h == HALVES - 1))
                m.then_inc(part, 1)
                with pe.Fori(0, GROUPS // 2) as i:
                    for s in range(2):
                        g = 2 * i + s
                        pe.wait_ge(fused_done, g + 1)
                        for t in range(TERMS):
                            pe.wait_ge(active, g * TERMS + t + 1)
                            m = nc.tensor.matmul(fuse_ps[s][:], fuse_w[:, t, :], y_in[s][t][:],
                                                 start=(t == 0), stop=(t == TERMS - 1))
                        m.then_inc(multiplied, 1)

            @block.vector
            def _(dve):
                with dve.Fori(0, GROUPS) as g:
                    dve.wait_ge(fused_done, g + 3)
                    nc.vector.bn_stats(stats_f[:, bass.ds(g, 1), :].rearrange("p g k -> p (g k)"),
                                       fused[:, bass.ds(g * SPAN, SPAN)]).then_inc(counted, 1)
                dve.wait_ge(counted, GROUPS)
                for b in range(B):
                    nc.vector.bn_aggr(mv[:], stats_f[:, b * GPB:(b + 1) * GPB, :].rearrange("p g k -> p (g k)"))\
                        .then_inc(counted, 1)
                    dve.wait_ge(counted, GROUPS + 3 * b + 1)
                    nc.vector.tensor_copy(mean_f[:, b:b + 1], mv[:, 0:1]).then_inc(counted, 1)
                    nc.vector.tensor_copy(var_f[:, b:b + 1], mv[:, 1:2]).then_inc(counted, 1)
                    dve.wait_ge(counted, GROUPS + 3 * b + 3)

        group_moments(nc, "gf", average_f, mean_f, var_f, gamma_f, beta_f, scale_f, shift_f, B, EPS_GN)

        with ExitStack() as c2:
            sb2, _, sem2 = tools(nc, c2, "f3")
            x_in = [sb2(f"x_in{q}", [P, L // 2]) for q in range(2 * B)]
            x_loaded = [sem2(f"x_loaded{q}") for q in range(2 * B)]
            active = sem2("active")
            added = sem2("added")
            stored = sem2("stored")
            block = c2.enter_context(nc.Block())
            parts = [(b, slice(k * (L // 2), (k + 1) * (L // 2))) for b in range(B) for k in range(2)]

            @block.sync
            def _(sp):
                for q, (b, px) in enumerate(parts):
                    sp.dma_start(x_in[q][:], x_dram[b, :, px]).then_inc(x_loaded[q], 16)
                for q, (b, px) in enumerate(parts):
                    sp.wait_ge(added, q + 1)
                    sp.dma_start(out_dram[b, :, px], x_in[q][:]).then_inc(stored, 16)
                sp.wait_ge(stored, 16 * len(parts))

            @block.scalar
            def _(act):
                for q, (b, px) in enumerate(parts):
                    f = fused[:, q * (L // 2):(q + 1) * (L // 2)]
                    nc.scalar.activation(f, f, ACT.Relu, bias=shift_f[:, b:b + 1],
                                         scale=scale_f[:, b:b + 1]).then_inc(active, 1)

            @block.vector
            def _(dve):
                for q in range(len(parts)):
                    dve.wait_ge(active, q + 1)
                    dve.wait_ge(x_loaded[q], 16)
                    nc.vector.tensor_tensor(x_in[q][:], x_in[q][:], fused[:, q * (L // 2):(q + 1) * (L // 2)],
                                            ALU.add).then_inc(added, 1)



def layer0_conv(nc, d, ident, x1):
    table = nc.dram_tensor("corner_table", [B * QROWS, 4 * P], F32, kind="Internal").ap()
    strips = nc.dram_tensor("strips", [GROUPS + 2, P, STRIP_ROWS, PADDED], F32, kind="Internal").ap()
    y_dram = [nc.dram_tensor(f"y_{n}", [B, HALVES, P, L], F32, kind="Internal").ap() for n, _ in BRANCHES]
    with ExitStack() as ctx:
        sb, _, _ = tools(nc, ctx, "l0")
        stats_sb = sb("stats", [P, len(BRANCHES), HALVES, (GROUPS + 1) * 6])
        mean_sb = sb("mean", [P, B])
        with ExitStack() as c1:
            sb1, _, _ = tools(nc, c1, "nrm")
            xpad = sb1("xpad", [P, B, PADDED, PADDED])
            with ExitStack() as c2:
                sb2, _, _ = tools(nc, c2, "tk")
                tok_sb = sb2("tok", [P, TILES, P])
                clear(nc, "cx", xpad)
                layer_norm(nc, "ln0", ident, d["x"], tok_sb, 1e-6,
                           lambda b, g: xpad[:, b, bass.ds(g * (SPAN // W) + HALO, SPAN // W), HALO:HALO + W])
                corner_table(nc, tok_sb, table)
            keep_strips(nc, xpad, strips, mean_sb)
        sweep(nc)
        deformable(nc, ident, table, strips, (d["ow4"], d["ow3"], d["ow1"], d["ow2"]), d["ob"], d["base"], d["rowb"],
                   d["tap_w"], y_dram, stats_sb)
        fuse(nc, d, y_dram, stats_sb, mean_sb, d["x"], x1)
    sweep(nc)


EXPERTS = 8


def mixture(nc, d, ident, x_dram, norm_sb, out_dram):
    E = EXPERTS
    with ExitStack() as ctx:
        sb, pb, sem = tools(nc, ctx, "mx")
        expert_w = sb("expert_w", [P, E * P])
        expert_b = sb("expert_b", [E, P])
        router_w = sb("router_w", [P, E])
        router_b = sb("router_b", [1, E])
        ones = sb("ones", [1, P])
        number = sb("number", [P, E])
        xn = [sb(f"xn{s}", [P, SPAN]) for s in range(2)]
        x_in = [sb(f"x_in{s}", [P, SPAN]) for s in range(2)]
        top_at = sb("top_at", [P, TPG, 8], mybir.dt.uint32)
        peak = sb("peak", [P, TPG])
        z = sb("z", [P, TPG, E])
        ez = sb("ez", [P, TPG, E])
        total = sb("total", [P, TPG])
        prob = sb("prob", [P, TPG, E])
        top = sb("top", [P, TPG, 8])
        at = sb("at", [P, TPG, 2])
        share = sb("share", [P, TPG, 2])
        pick = sb("pick", [P, TPG, E])
        gate = sb("gate", [P, TPG, E])
        gate_t = sb("gate_t", [E, SPAN])
        product = sb("product", [P, E, P])
        mixed = sb("mixed", [P, TPG, P])
        summed = sb("summed", [P, TPG, P])
        route_ps = pb("route_ps", [P, 512])
        gate_ps = pb("gate_ps", [P, 512])
        bias_ps = pb("bias_ps", [P, TPG, P])
        out_ps = pb("out_ps", [P, SPAN])
        expert_ps = [pb(f"expert_ps{s}", [P, E, P]) for s in range(2)]
        loaded = sem("loaded")
        ones_set = sem("ones_set")
        xn_ready = sem("xn_ready")
        x_loaded = [sem(f"x_loaded{s}") for s in range(2)]
        routed = sem("routed")
        route_free = sem("route_free")
        shifted = sem("shifted")
        exped = sem("exped")
        topped = sem("topped")
        gated = sem("gated")
        gate_turned = sem("gate_turned")
        gate_kept = sem("gate_kept")
        experted = sem("experted")
        expert_free = sem("expert_free")
        biased = sem("biased")
        mixed_done = sem("mixed_done")
        out_turned = sem("out_turned")
        out_added = sem("out_added")
        stored = [sem(f"stored{s}") for s in range(2)]
        steps = sem("steps")
        PER = 13 + 4 * TPG
        block = ctx.enter_context(nc.Block())

        @block.sync
        def _(sp):
            for dst, src in ((expert_w, "expert_w"), (expert_b, "expert_b"), (router_w, "router_w"),
                             (router_b, "router_b"), (number, "expert_number")):
                sp.dma_start(dst[:], d[src]).then_inc(loaded, 16)
            for s in range(2):
                sp.dma_start(x_in[s][:], x_dram[0, :, s * SPAN:(s + 1) * SPAN]).then_inc(x_loaded[s], 16)

            def turn_over(b, gl, s, ahead):
                sp.wait_ge(out_added, b * GPB + gl + 1)
                sp.dma_start(out_dram[b, :, bass.ds(gl * SPAN, SPAN)], x_in[s][:]).then_inc(stored[s], 16)
                sp.wait_ge(stored[s], (b * GPB + gl + 2 - s) * 8)
                if ahead is not None:
                    nb, ngl = ahead
                    sp.dma_start(x_in[s][:], x_dram[nb, :, bass.ds(ngl * SPAN, SPAN)]).then_inc(x_loaded[s], 16)

            for b in range(B):
                with sp.Fori(0, GPB // 2 - 1) as i:
                    for s in range(2):
                        turn_over(b, 2 * i + s, s, (b, 2 * i + s + 2))
                for s in range(2):
                    turn_over(b, GPB - 2 + s, s, (b + 1, s) if b + 1 < B else None)

        @block.gpsimd
        def _(pool):
            def stage(g, s):
                nc.gpsimd.tensor_copy(xn[s][:], norm_sb[:, bass.ds(g * SPAN, SPAN)]).then_inc(xn_ready, 1)

            stage(0, 0)
            stage(1, 1)
            for b in range(B):
                with pool.Fori(0, GPB // 2 - (1 if b == 0 else 0)) as i:
                    for s in range(2):
                        gl = 2 * i + s + (2 if b == 0 else 0)
                        g = b * GPB + gl
                        pool.wait_ge(out_turned, g - 1)
                        stage(g, s)

        @block.tensor
        def _(pe):
            pe.wait_ge(loaded, 16 * 5)
            pe.wait_ge(ones_set, 1)

            def route(g, s):
                pe.wait_ge(xn_ready, g + 1)
                pe.wait_ge(route_free, g + 1)
                for j in range(TPG):
                    cols = route_ps[:, j * E:(j + 1) * E]
                    nc.tensor.matmul(cols, ones[:], router_b[:], start=True, stop=False)
                    m = nc.tensor.matmul(cols, xn[s][:, j * TILE:(j + 1) * TILE], router_w[:], start=False, stop=True)
                m.then_inc(routed, 1)

            def experts(g, s, j):
                t = g * TPG + j
                pe.wait_ge(expert_free, t + 1)
                for h in range(2):
                    m = nc.tensor.matmul(expert_ps[j % 2][:, h * (E // 2):(h + 1) * (E // 2), :],
                                         xn[s][:, j * TILE:(j + 1) * TILE],
                                         expert_w[:, h * 512:(h + 1) * 512], start=True, stop=True)
                m.then_inc(experted, 1)

            def rest(g, s):
                experts(g, s, 0)
                experts(g, s, 1)
                pe.wait_ge(gated, g + 1)
                for j in range(TPG):
                    m = nc.tensor.transpose(gate_ps[0:E, j * TILE:(j + 1) * TILE], gate[:, j, :], ident[:])
                m.then_inc(gate_turned, 1)
                pe.wait_ge(gate_kept, g + 1)
                for j in range(TPG):
                    m = nc.tensor.matmul(bias_ps[:, j, :], gate_t[:, j * TILE:(j + 1) * TILE], expert_b[:],
                                         start=True, stop=True)
                m.then_inc(biased, 1)
                experts(g, s, 2)
                experts(g, s, 3)

            def turn_out(g):
                pe.wait_ge(mixed_done, g + 1)
                for j in range(TPG):
                    m = nc.tensor.transpose(out_ps[:, j * TILE:(j + 1) * TILE], summed[:, j, :], ident[:])
                m.then_inc(out_turned, 1)

            route(0, 0)
            with pe.Fori(0, GROUPS // 2 - 1) as i:
                rest(2 * i, 0)
                route(2 * i + 1, 1)
                turn_out(2 * i)
                rest(2 * i + 1, 1)
                turn_out(2 * i + 1)
                route(2 * i + 2, 0)
            rest(GROUPS - 2, 0)
            route(GROUPS - 1, 1)
            turn_out(GROUPS - 2)
            rest(GROUPS - 1, 1)
            turn_out(GROUPS - 1)

        @block.scalar
        def _(act):
            with act.Fori(0, GROUPS) as g:
                act.wait_ge(shifted, g + 1)
                nc.scalar.activation(ez[:], z[:], ACT.Exp).then_inc(exped, 1)
                act.wait_ge(gate_turned, g + 1)
                nc.scalar.activation(gate_t[:], gate_ps[0:E, :], ACT.Copy).then_inc(gate_kept, 1)

        @block.vector
        def _(dve):
            v = nc.vector
            v.memset(ones[:], 1.0).then_inc(ones_set, 1)
            dve.sem_inc(route_free, 1)
            dve.sem_inc(expert_free, 2)
            dve.wait_ge(loaded, 16 * 5)

            def every(ap):
                return ap.unsqueeze(2).broadcast_to([P, TPG, E])

            with dve.Fori(0, GROUPS // 2) as i:
                for s in range(2):
                    g = 2 * i + s
                    own = Tally(dve, steps, g * PER)
                    logits = route_ps[:, 0:TPG * E].rearrange("p (j e) -> p j e", e=E)
                    dve.wait_ge(routed, g + 1)
                    own.done(v.tensor_reduce(peak[:], logits, AX_X, ALU.max))
                    own.settle()
                    own.done(v.tensor_tensor(z[:], logits, every(peak[:]), ALU.subtract))
                    own.settle()
                    dve.sem_inc(route_free, 1)
                    dve.sem_inc(shifted, 1)
                    dve.wait_ge(exped, g + 1)
                    own.done(v.tensor_reduce(total[:], ez[:], AX_X, ALU.add))
                    own.settle()
                    own.done(v.reciprocal(total[:], total[:]))
                    own.settle()
                    own.done(v.tensor_tensor(prob[:], ez[:], every(total[:]), ALU.mult))
                    own.settle()
                    dve.sem_inc(topped, 1)
                    for j in range(TPG):
                        own.done(v.max(top[:, j, :], prob[:, j, :]))
                    own.settle()
                    dve.sem_inc(topped, 1)
                    for j in range(TPG):
                        own.done(v.max_index(top_at[:, j, :], top[:, j, :], prob[:, j, :]))
                    own.settle()
                    own.done(v.tensor_copy(at[:], top_at[:, :, 0:2]))
                    own.done(v.tensor_reduce(peak[:], top[:, :, 0:2], AX_X, ALU.add))
                    own.settle()
                    own.done(v.reciprocal(peak[:], peak[:]))
                    own.settle()
                    own.done(v.tensor_tensor(share[:], top[:, :, 0:2],
                                             peak[:].unsqueeze(2).broadcast_to([P, TPG, 2]), ALU.mult))
                    numbers = number[:].unsqueeze(1).broadcast_to([P, TPG, E])
                    own.done(v.tensor_tensor(gate[:], numbers, every(at[:, :, 0]), ALU.is_equal))
                    own.done(v.tensor_tensor(pick[:], numbers, every(at[:, :, 1]), ALU.is_equal))
                    own.settle()
                    own.done(v.tensor_tensor(gate[:], gate[:], every(share[:, :, 0]), ALU.mult))
                    own.done(v.tensor_tensor(pick[:], pick[:], every(share[:, :, 1]), ALU.mult))
                    own.settle()
                    v.tensor_tensor(gate[:], gate[:], pick[:], ALU.add).then_inc(gated, 1)
                    dve.wait_ge(gated, g + 1)
                    for j in range(TPG):
                        dve.wait_ge(experted, g * TPG + j + 1)
                        own.done(v.tensor_tensor(product[:], expert_ps[j % 2][:],
                                                 gate[:, j, :].unsqueeze(2).broadcast_to([P, E, P]), ALU.mult))
                        own.settle()
                        dve.sem_inc(expert_free, 1)
                        own.done(v.tensor_reduce(mixed[:, j, :], product[:].rearrange("p e c -> p c e"), AX_X,
                                                 ALU.add))
                        own.settle()
                    dve.wait_ge(biased, g + 1)
                    v.tensor_tensor(summed[:], mixed[:], bias_ps[:], ALU.add).then_inc(mixed_done, 1)
                    dve.wait_ge(out_turned, g + 1)
                    dve.wait_ge(x_loaded[s], (i + 1) * 16)
                    v.tensor_tensor(x_in[s][:], x_in[s][:], out_ps[:], ALU.add).then_inc(out_added, 1)
                    dve.wait_ge(out_added, g + 1)
                    assert own.n == PER, own.n



def layer0_ffn(nc, d, ident, x1, x2):
    with ExitStack() as ctx:
        sb, _, _ = tools(nc, ctx, "l0f")
        norm_sb = sb("norm", [P, N])
        tok_sb = sb("tok", [P, TILES, P])
        layer_norm(nc, "ln1", ident, x1, tok_sb, 1e-5,
                   lambda b, g: norm_sb[:, bass.ds((b * GPB + g) * SPAN, SPAN)])
        mixture(nc, d, ident, x1, norm_sb, x2)
    sweep(nc)


DI = 2 * P
ZX = 2 * DI // P
DWK = 5
DWH = DWK // 2
DWP = H + 2 * DWH
STATES = 16
DT_RANK = 8
CONV1 = 4
SPATIAL = 7
PE_TAPS = 11


def project_and_filter(nc, d, ident, norm_sb, u_dram, total_sb, peak_sb, ztotal_sb, zpeak_sb):
    taps = [(ky, kx) for ky in range(DWK) for kx in range(DWK)]
    pe_taps, v_taps = taps[:PE_TAPS], taps[PE_TAPS:]
    NV = len(v_taps)
    ROWS = SPAN // W
    ITEMS = [(blk, b) for blk in range(ZX) for b in range(B)]
    with ExitStack() as ctx:
        sb, pb, sem = tools(nc, ctx, "dw")
        in_w = sb("in_w", [P, ZX * P])
        dw_w = sb("dw_w", [P, ZX, DWK * DWK])
        diag = [sb(f"diag{s}", [P, PE_TAPS, P]) for s in range(2)]
        padded = [sb(f"padded{s}", [P, DWP, DWP]) for s in range(2)]
        u = [sb(f"u{s}", [P, SPAN]) for s in range(4)]
        proj_ps = [pb(f"proj_ps{s}", [P, SPAN]) for s in range(2)]
        conv_ps = [pb(f"conv_ps{s}", [P, SPAN]) for s in range(4)]
        turn_ps = [pb(f"turn_ps{s}", [P, TPG, P]) for s in range(2)]
        loaded = sem("loaded")
        cleared = sem("cleared")
        projected = sem("projected")
        placed = sem("placed")
        diagonals = sem("diagonals")
        item_done = sem("item_done")
        conv_done = sem("conv_done")
        conv_read = sem("conv_read")
        filtered = sem("filtered")
        stored = [sem(f"stored{s}") for s in range(4)]
        u_free = sem("u_free")
        turned = sem("turned")
        steps = sem("steps")
        block = ctx.enter_context(nc.Block())

        @block.sync
        def _(sp):
            sp.dma_start(in_w[:], d["in_w"]).then_inc(loaded, 16)
            sp.dma_start(dw_w[:], d["dw_w"]).then_inc(loaded, 16)
            sp.sem_inc(u_free, 4)
            for n, (blk, b) in enumerate(ITEMS):
                with sp.Fori(0, GPB // 4) as i:
                    for s in range(4):
                        c = 4 * i + s
                        sp.wait_ge(filtered, n * GPB + c + 1)
                        sp.dma_start(u_dram[blk, b, :, bass.ds(c * SPAN, SPAN)], u[s][:]).then_inc(stored[s], 16)
                        sp.wait_ge(stored[s], (n * (GPB // 4) + i + 1) * 16)
                        sp.sem_inc(u_free, 1)

        @block.gpsimd
        def _(pool):
            for s in range(2):
                nc.gpsimd.memset(padded[s][:], 0.0).then_inc(cleared, 1)

        @block.tensor
        def _(pe):
            pe.wait_ge(loaded, 32)

            def project(n, c, s):
                blk, b = ITEMS[n]
                pe.wait_ge(placed, n * GPB + c + 1)
                nc.tensor.matmul(proj_ps[s][:], in_w[:, blk * P:(blk + 1) * P],
                                 norm_sb[:, bass.ds(b * L + c * SPAN, SPAN)], start=True, stop=True)\
                    .then_inc(projected, 1)

            def convolve(n, c, s):
                pe.wait_ge(conv_read, n * GPB + c + 1)
                for k, (ky, kx) in enumerate(pe_taps):
                    m = nc.tensor.matmul(conv_ps[s][:], diag[ITEMS[n][0] % 2][:, k, :],
                                         padded[n % 2][:, bass.ds(c * ROWS + ky, ROWS), kx:kx + W],
                                         start=(k == 0), stop=(k == PE_TAPS - 1))
                m.then_inc(conv_done, 1)

            def turn(n, c, s):
                if ITEMS[n][0] < ZX // 2:
                    return
                pe.wait_ge(filtered, n * GPB + c + 1)
                for j in range(TPG):
                    m = nc.tensor.transpose(turn_ps[s % 2][:, j, :], u[s][:, j * TILE:(j + 1) * TILE], ident[:])
                m.then_inc(turned, 1)

            pe.wait_ge(cleared, 2)
            pe.wait_ge(item_done, 1)
            with pe.Fori(0, GPB // 2) as i:
                for s in range(2):
                    project(0, 2 * i + s, s)
            for n in range(len(ITEMS)):
                pe.wait_ge(placed, (n + 1) * GPB + 2)
                pe.wait_ge(diagonals, (ITEMS[n][0] + 1) * PE_TAPS)
                if n + 1 < len(ITEMS):
                    pe.wait_ge(item_done, n + 2)
                with pe.Fori(0, GPB // 4) as i:
                    for pair in range(2):
                        for s in (2 * pair, 2 * pair + 1):
                            convolve(n, 4 * i + s, s)
                            if n + 1 < len(ITEMS):
                                project(n + 1, 4 * i + s, s % 2)
                        for s in (2 * pair, 2 * pair + 1):
                            turn(n, 4 * i + s, s)

        @block.scalar
        def _(act):
            act.wait_ge(loaded, 32)
            act.wait_ge(cleared, 2)
            act.sem_inc(placed, 2)

            def place(n, c, s):
                act.wait_ge(projected, n * GPB + c + 1)
                nc.scalar.activation(padded[n % 2][:, bass.ds(DWH + c * ROWS, ROWS), DWH:DWH + W],
                                     proj_ps[s][:].rearrange("p (r c) -> p r c", c=W), ACT.Copy).then_inc(placed, 1)

            for n, (blk, b) in enumerate(ITEMS):
                if b == 0:
                    act.wait_ge(item_done, max(1, B * (blk - 1) + 2))
                    for k, (ky, kx) in enumerate(pe_taps):
                        t = ky * DWK + kx
                        nc.scalar.activation(diag[blk % 2][:, k, :], ident[:], ACT.Copy,
                                             scale=dw_w[:, blk, t:t + 1]).then_inc(diagonals, 1)
                with act.Fori(0, GPB // 2) as i:
                    for s in range(2):
                        place(n, 2 * i + s, s)

        @block.vector
        def _(dve):
            v = nc.vector
            dve.wait_ge(loaded, 32)
            dve.sem_inc(item_done, 2)
            dve.sem_inc(conv_read, 4)
            PER = 2 * (NV + 3)
            for n, (blk, b) in enumerate(ITEMS):
                dve.wait_ge(placed, (n + 1) * GPB + 2)
                with dve.Fori(0, GPB // 4) as i:
                    for pair in range(2):
                        own = Tally(dve, steps, (n * (GPB // 2) + 2 * i + pair) * PER)
                        slots = (2 * pair, 2 * pair + 1)
                        for k, (ky, kx) in enumerate(v_taps):
                            t = ky * DWK + kx
                            for s in slots:
                                c = 4 * i + s
                                rows = padded[n % 2][:, bass.ds(c * ROWS + ky, ROWS), kx:kx + W]
                                w = dw_w[:, blk, t:t + 1]
                                image = u[s][:].rearrange("p (r c) -> p r c", c=W)
                                if k == 0:
                                    dve.wait_ge(u_free, n * GPB + c + 1)
                                    own.done(v.tensor_scalar(image, rows, w, None, ALU.mult))
                                else:
                                    dve.wait_ge(steps, own.base + own.n - 1)
                                    own.done(v.scalar_tensor_tensor(out=image, in0=rows, scalar=w, in1=image,
                                                                    op0=ALU.mult, op1=ALU.add))
                        for s in slots:
                            dve.wait_ge(steps, own.base + own.n - 1)
                            dve.wait_ge(conv_done, n * GPB + 4 * i + s + 1)
                            own.done(v.tensor_tensor(u[s][:], u[s][:], conv_ps[s][:], ALU.add))
                        own.settle()
                        dve.sem_inc(conv_read, 2)
                        dve.sem_inc(filtered, 2)
                        for s in slots:
                            c = 4 * i + s
                            if blk < ZX // 2:
                                own.done(v.tensor_reduce(total_sb[:, blk, b, bass.ds(c, 1)], u[s][:], AX_X, ALU.add))
                                own.done(v.tensor_reduce(peak_sb[:, blk, b, bass.ds(c, 1)], u[s][:], AX_X, ALU.max))
                            else:
                                z = blk - ZX // 2
                                tile = bass.ds(b * (TILES // B) + c * TPG, TPG)
                                dve.wait_ge(turned, (n - ZX // 2 * B) * GPB + c + 1)
                                own.done(v.tensor_reduce(ztotal_sb[:, z, tile], turn_ps[s % 2][:], AX_X, ALU.add))
                                own.done(v.tensor_reduce(zpeak_sb[:, z, tile], turn_ps[s % 2][:], AX_X, ALU.max))
                        own.settle()
                        assert own.n == PER
                dve.sem_inc(item_done, 1)


def attention(nc, d, ident, total_sb, peak_sb, ztotal_sb, zpeak_sb, conv1_sb, zs_dram, gate_dram):
    RED = DI // 16
    with ExitStack() as ctx:
        sb, pb, sem = tools(nc, ctx, "at")
        fc1 = sb("fc1", [P, HALVES, RED])
        fc2 = sb("fc2", [RED, DI])
        conv1_w = sb("conv1_w", [P, HALVES, CONV1])
        spatial_w = sb("spatial_w", [TILES, 2 * SPATIAL])
        pooled = sb("pooled", [P, HALVES, 2, B])
        hidden = sb("hidden", [RED, 2, B])
        both = sb("both", [RED, B])
        channel = sb("channel", [P, HALVES, B])
        zmean = sb("zmean", [P, TILES])
        zmax = sb("zmax", [P, TILES])
        rows = sb("rows", [TILES, 2, P])
        zeros = sb("zeros", [2 * B, SPATIAL // 2])
        window = sb("window", [TILES, 2, P + SPATIAL - 1])
        acc = sb("acc", [TILES, P])
        gate = sb("gate", [TILES, P])
        ps = [pb(f"ps{i}", [P, 512]) for i in range(5)]
        loaded = sem("loaded")
        steps = sem("steps")
        pool_done = sem("pool_done")
        product = sem("product")
        hidden_done = sem("hidden_done")
        both_done = sem("both_done")
        channel_done = sem("channel_done")
        zready = sem("zready")
        zturned = sem("zturned")
        rows_done = sem("rows_done")
        written = sem("written")
        windowed = sem("windowed")
        summed = sem("summed")
        gate_done = sem("gate_done")
        block = ctx.enter_context(nc.Block())
        half = SPATIAL // 2

        @block.sync
        def _(sp):
            for dst, src in ((fc1, d["fc1"]), (fc2, d["fc2"]), (conv1_w, d["conv1_w"]),
                             (spatial_w, d["spatial_w"].partition_broadcast(TILES))):
                sp.dma_start(dst[:], src).then_inc(loaded, 16)
            sp.wait_ge(zready, 3)
            sides = zs_dram.rearrange("k b n -> (k b) n")
            sp.dma_start(sides[:, 0:half], zeros[:]).then_inc(written, 16)
            sp.dma_start(sides[:, half + L:], zeros[:]).then_inc(written, 16)
            sp.wait_ge(rows_done, 2)
            for k in range(2):
                for b in range(B):
                    t0 = b * (TILES // B)
                    sp.dma_start(zs_dram[k, b, half:half + L].rearrange("(t p) -> t p", p=P),
                                 rows[t0:t0 + TILES // B, k, :]).then_inc(written, 16)
            sp.wait_ge(written, 16 * (2 + 2 * B))
            for k in range(2):
                for b in range(B):
                    t0 = b * (TILES // B)
                    at = zs_dram[k, b]
                    src = bass.AP(tensor=at.tensor, offset=at.offset, ap=[[P, TILES // B], [1, P + SPATIAL - 1]])
                    sp.dma_start(window[t0:t0 + TILES // B, k, :], src).then_inc(windowed, 16)
            sp.wait_ge(gate_done, 1)
            sp.dma_start(gate_dram.rearrange("b (t p) -> (b t) p", p=P), gate[:]).then_inc(written, 16)
            sp.wait_ge(written, 16 * (3 + 2 * B))

        @block.tensor
        def _(pe):
            pe.wait_ge(zready, 3)
            nc.tensor.transpose(ps[2][0:TILES, 0:P], zmean[:], ident[:]).then_inc(zturned, 1)
            nc.tensor.transpose(ps[3][0:TILES, 0:P], zmax[:], ident[:]).then_inc(zturned, 1)
            pe.wait_ge(loaded, 16 * 4)
            pe.wait_ge(pool_done, 1)
            for h in range(HALVES):
                m = nc.tensor.matmul(ps[0][0:RED, 0:2 * B], fc1[:, h, :], pooled[:, h].rearrange("p k b -> p (k b)"),
                                     start=(h == 0), stop=(h == HALVES - 1))
            m.then_inc(product, 1)
            pe.wait_ge(both_done, 1)
            for h in range(HALVES):
                m = nc.tensor.matmul(ps[1][:, h * B:(h + 1) * B], fc2[:, h * P:(h + 1) * P], both[:],
                                     start=True, stop=True)
            m.then_inc(product, 1)

        @block.scalar
        def _(act):
            act.wait_ge(zturned, 2)
            for k in range(2):
                nc.scalar.activation(rows[:, k, :], ps[2 + k][0:TILES, 0:P], ACT.Copy).then_inc(rows_done, 1)
            act.wait_ge(product, 1)
            nc.scalar.activation(hidden[:].rearrange("p k b -> p (k b)"), ps[0][0:RED, 0:2 * B],
                                 ACT.Silu).then_inc(hidden_done, 1)
            act.wait_ge(product, 2)
            nc.scalar.activation(channel[:].rearrange("p h b -> p (h b)"), ps[1][:, 0:HALVES * B],
                                 ACT.Sigmoid).then_inc(channel_done, 1)
            act.wait_ge(summed, 2 * SPATIAL)
            nc.scalar.activation(gate[:], acc[:], ACT.Sigmoid).then_inc(gate_done, 1)

        @block.vector
        def _(dve):
            v = nc.vector
            own = Tally(dve, steps)
            v.memset(zeros[:], 0.0).then_inc(zready, 1)
            own.done(v.tensor_tensor(zmean[:], ztotal_sb[:, 0, :], ztotal_sb[:, 1, :], ALU.add))
            own.settle()
            v.tensor_scalar(zmean[:], zmean[:], 1.0 / DI, None, ALU.mult).then_inc(zready, 1)
            v.tensor_tensor(zmax[:], zpeak_sb[:, 0, :], zpeak_sb[:, 1, :], ALU.max).then_inc(zready, 1)
            for h in range(HALVES):
                own.done(v.tensor_reduce(pooled[:, h, 0, :], total_sb[:, h], AX_X, ALU.add))
                own.done(v.tensor_reduce(pooled[:, h, 1, :], peak_sb[:, h], AX_X, ALU.max))
            own.settle()
            v.tensor_scalar(pooled[:, :, 0, :], pooled[:, :, 0, :], 1.0 / L, None, ALU.mult).then_inc(pool_done, 1)
            dve.wait_ge(hidden_done, 1)
            v.tensor_tensor(both[:], hidden[:, 0, :], hidden[:, 1, :], ALU.add).then_inc(both_done, 1)
            dve.wait_ge(channel_done, 1)
            dve.wait_ge(loaded, 16 * 4)
            for h in range(HALVES):
                for b in range(B):
                    own.done(v.tensor_scalar(conv1_sb[:, h, b, :], conv1_w[:, h, :], channel[:, h, b:b + 1], None,
                                             ALU.mult))
            dve.wait_ge(windowed, 16 * 2 * B)
            for n in range(2 * SPATIAL):
                k, tap = n // SPATIAL, n % SPATIAL
                src = window[:, k, tap:tap + P]
                if n == 0:
                    v.tensor_scalar(acc[:], src, spatial_w[:, 0:1], None, ALU.mult).then_inc(summed, 1)
                else:
                    dve.wait_ge(summed, n)
                    v.scalar_tensor_tensor(out=acc[:], in0=src, scalar=spatial_w[:, n:n + 1], in1=acc[:],
                                           op0=ALU.mult, op1=ALU.add).then_inc(summed, 1)
            own.settle()


def causal(nc, tag, d, b, u_dram, conv1_sb, xs_sb):
    with ExitStack() as ctx:
        sb, _, sem = tools(nc, ctx, tag)
        u = [sb(f"u{h}", [P, CONV1 - 1 + L]) for h in range(HALVES)]
        bias = sb("bias", [P, HALVES])
        loaded = [sem(f"loaded{h}") for h in range(HALVES)]
        cleared = sem("cleared")
        steps = sem("steps")
        summed = sem("summed")
        active = sem("active")
        PARTS = 4
        LP = L // PARTS
        block = ctx.enter_context(nc.Block())

        @block.sync
        def _(sp):
            for h in range(HALVES):
                sp.dma_start(u[h][:, CONV1 - 1:], u_dram[h, b]).then_inc(loaded[h], 16)
            sp.dma_start(bias[:], d["conv1_b"]).then_inc(loaded[0], 16)

        @block.vector
        def _(dve):
            for h in range(HALVES):
                nc.vector.memset(u[h][:, 0:CONV1 - 1], 0.0).then_inc(cleared, 1)
            dve.wait_ge(cleared, HALVES)
            n = 0
            for h in range(HALVES):
                dve.wait_ge(loaded[h], 32 if h == 0 else 16)
                for k in range(CONV1):
                    for q in range(PARTS):
                        src = u[h][:, q * LP + k:q * LP + k + LP]
                        dst = xs_sb[:, h, q * LP:(q + 1) * LP]
                        w = conv1_sb[:, h, b, k:k + 1]
                        if k == 0:
                            ins = nc.vector.tensor_scalar(dst, src, w, None, ALU.mult)
                        else:
                            dve.wait_ge(steps, n - PARTS + 1)
                            ins = nc.vector.scalar_tensor_tensor(out=dst, in0=src, scalar=w, in1=dst,
                                                                 op0=ALU.mult, op1=ALU.add)
                        ins.then_inc(steps, 1)
                        n += 1

        @block.scalar
        def _(act):
            act.wait_ge(loaded[0], 32)
            for h in range(HALVES):
                for q in range(PARTS):
                    act.wait_ge(steps, h * CONV1 * PARTS + (CONV1 - 1) * PARTS + q + 1)
                    part = xs_sb[:, h, q * LP:(q + 1) * LP]
                    nc.scalar.activation(part, part, ACT.Silu, bias=bias[:, h:h + 1]).then_inc(active, 1)


def step_sizes(nc, tag, d, b, xs_sb, delta_sb, du_sb, bc_dram):
    SERIES = (1.0 / 5, -1.0 / 4, 1.0 / 3, -1.0 / 2, 1.0)
    LIMIT = 2.0 ** -5
    with ExitStack() as ctx:
        sb, pb, sem = tools(nc, ctx, tag)
        xproj = sb("xproj", [P, HALVES, DT_RANK + 2 * STATES])
        dtproj = sb("dtproj", [DT_RANK, DI])
        bias = sb("bias", [P, HALVES])
        one = sb("one", [P, 1])
        low = sb("low", [DT_RANK, SPAN])
        bc = [sb(f"bc{s}", [2 * STATES, SPAN]) for s in range(2)]
        v_sb = [sb(f"v{h}", [P, SPAN]) for h in range(HALVES)]
        e_sb = [sb(f"e{h}", [P, SPAN]) for h in range(HALVES)]
        ln_sb = [sb(f"ln{h}", [P, SPAN]) for h in range(HALVES)]
        poly = [sb(f"poly{h}", [P, SPAN]) for h in range(HALVES)]
        large = [sb(f"large{h}", [P, SPAN], I32) for h in range(HALVES)]
        low_ps = pb("low_ps", [P, SPAN])
        bc_ps = pb("bc_ps", [P, SPAN])
        delta_ps = [pb(f"delta_ps{h}", [P, SPAN]) for h in range(HALVES)]
        loaded = sem("loaded")
        one_set = sem("one_set")
        lowered = sem("lowered")
        bc_done = sem("bc_done")
        kept = sem("kept")
        bc_kept = sem("bc_kept")
        bc_read = sem("bc_read")
        stored = sem("stored")
        bc_free = sem("bc_free")
        spread = sem("spread")
        v_read = sem("v_read")
        logged = sem("logged")
        compared = sem("compared")
        done = sem("done")
        steps = sem("steps")
        ACTS = 4
        acts = sem("acts")
        PER = 2 * (len(SERIES) + 4)
        block = ctx.enter_context(nc.Block())

        @block.sync
        def _(sp):
            sp.dma_start(xproj[:], d["xproj"]).then_inc(loaded, 16)
            sp.dma_start(dtproj[:], d["dtproj"]).then_inc(loaded, 16)
            sp.dma_start(bias[:], d["dt_b"]).then_inc(loaded, 16)
            sp.sem_inc(bc_free, 2)
            with sp.Fori(0, GPB // 2) as i:
                for s in range(2):
                    c = 2 * i + s
                    sp.wait_ge(bc_kept, c + 1)
                    sp.dma_start(bc_dram[b, :, bass.ds(c * SPAN, SPAN)], bc[s][:]).then_inc(stored, 16)
                    sp.wait_ge(stored, (c + 1) * 16)
                    sp.sem_inc(bc_free, 1)

        @block.tensor
        def _(pe):
            pe.wait_ge(loaded, 16 * 3)
            pe.sem_inc(spread, 2)
            with pe.Fori(0, GPB) as c:
                pe.wait_ge(bc_read, c + 1)
                for h in range(HALVES):
                    xs = xs_sb[:, h, bass.ds(c * SPAN, SPAN)]
                    m = nc.tensor.matmul(low_ps[0:DT_RANK, :], xproj[:, h, 0:DT_RANK], xs,
                                         start=(h == 0), stop=(h == HALVES - 1))
                m.then_inc(lowered, 1)
                for h in range(HALVES):
                    xs = xs_sb[:, h, bass.ds(c * SPAN, SPAN)]
                    m = nc.tensor.matmul(bc_ps[0:2 * STATES, :], xproj[:, h, DT_RANK:], xs,
                                         start=(h == 0), stop=(h == HALVES - 1))
                m.then_inc(bc_done, 1)
                pe.wait_ge(kept, c + 1)
                for h in range(HALVES):
                    pe.wait_ge(v_read, 2 * c + h + 1)
                    nc.tensor.matmul(delta_ps[h][:], dtproj[:, h * P:(h + 1) * P], low[:],
                                     start=True, stop=True).then_inc(spread, 1)

        @block.scalar
        def _(act):
            act.wait_ge(loaded, 16 * 3)
            act.wait_ge(one_set, 1)
            act.sem_inc(bc_read, 1)
            act.sem_inc(v_read, 2)
            with act.Fori(0, GPB // 2) as i:
                for s in range(2):
                    c = 2 * i + s
                    act.wait_ge(lowered, c + 1)
                    nc.scalar.activation(low[:], low_ps[0:DT_RANK, :], ACT.Copy).then_inc(kept, 1)
                    act.wait_ge(bc_done, c + 1)
                    act.wait_ge(bc_free, c + 1)
                    nc.scalar.activation(bc[s][:], bc_ps[0:2 * STATES, :], ACT.Copy).then_inc(bc_kept, 1)
                    act.wait_ge(bc_kept, c + 1)
                    act.sem_inc(bc_read, 1)
                    for h in range(HALVES):
                        n = 2 * c + h
                        act.wait_ge(spread, n + 3)
                        act.wait_ge(done, n + 1)
                        nc.scalar.activation(v_sb[h][:], delta_ps[h][:], ACT.Identity,
                                             bias=bias[:, h:h + 1]).then_inc(acts, 1)
                        nc.scalar.activation(e_sb[h][:], delta_ps[h][:], ACT.Abs,
                                             bias=bias[:, h:h + 1]).then_inc(acts, 1)
                    act.wait_ge(acts, ACTS * 2 * c + 4)
                    act.sem_inc(v_read, 2)
                    for h in range(HALVES):
                        nc.scalar.activation(e_sb[h][:], e_sb[h][:], ACT.Exp, scale=-1.0).then_inc(acts, 1)
                    act.wait_ge(acts, ACTS * 2 * c + 6)
                    for h in range(HALVES):
                        nc.scalar.activation(ln_sb[h][:], e_sb[h][:], ACT.Ln, bias=one[:]).then_inc(acts, 1)
                    act.wait_ge(acts, ACTS * 2 * c + 8)
                    act.sem_inc(logged, 2)

        @block.vector
        def _(dve):
            v = nc.vector
            v.memset(one[:], 1.0).then_inc(one_set, 1)
            dve.sem_inc(done, 2)
            with dve.Fori(0, GPB) as c:
                own = Tally(dve, steps, c * PER)
                both = range(HALVES)
                dve.wait_ge(logged, 2 * c + 2)
                for h in both:
                    own.done(v.tensor_scalar(poly[h][:], e_sb[h][:], SERIES[0], SERIES[1], ALU.mult, ALU.add))
                for term in (0.0, *SERIES[2:]):
                    own.settle()
                    for h in both:
                        own.done(v.scalar_tensor_tensor(out=poly[h][:], in0=poly[h][:], scalar=term, in1=e_sb[h][:],
                                                        op0=ALU.add, op1=ALU.mult))
                for h in both:
                    own.done(v.tensor_scalar(large[h][:], e_sb[h][:], LIMIT, None, ALU.is_ge))
                own.settle()
                dve.sem_inc(compared, 1)
                for h in both:
                    own.done(v.copy_predicated(poly[h][:], large[h][:], ln_sb[h][:]))
                own.settle()
                for h in both:
                    delta = delta_sb[:, h, bass.ds(c * SPAN, SPAN)]
                    own.done(v.scalar_tensor_tensor(out=delta, in0=v_sb[h][:], scalar=0.0, in1=poly[h][:],
                                                    op0=ALU.max, op1=ALU.add))
                own.settle()
                dve.sem_inc(done, 2)
                for h in both:
                    at = bass.ds(c * SPAN, SPAN)
                    own.done(v.tensor_tensor(du_sb[:, h, at], delta_sb[:, h, at], xs_sb[:, h, at], ALU.mult))
                own.settle()
                assert own.n == PER, own.n


CHUNK = 1024


def scan(nc, tag, d, b, ident, xs_sb, delta_sb, du_sb, y_sb, bc_dram):
    CHUNKS = L // CHUNK
    BANKS = CHUNK // 512
    with ExitStack() as ctx:
        sb, pb, sem = tools(nc, ctx, tag)
        a_log = sb("a_log", [P, HALVES, STATES])
        a_exp = sb("a_exp", [P, HALVES, STATES])
        a_sb = sb("a", [P, HALVES, STATES])
        skip = sb("skip", [P, HALVES])
        carry = sb("carry", [P, STATES, HALVES])
        b_row = [sb(f"b_row{s}", [P, CHUNK]) for s in range(2)]
        c_row = [sb(f"c_row{s}", [P, CHUNK]) for s in range(2)]
        decay = [sb(f"decay{h}", [P, CHUNK]) for h in range(HALVES)]
        drive = [sb(f"drive{h}", [P, CHUNK]) for h in range(HALVES)]
        state = [sb(f"state{h}", [P, CHUNK]) for h in range(HALVES)]
        read = [[sb(f"read{h}_{s}", [P, CHUNK]) for s in range(2)] for h in range(HALVES)]
        y_ps = [pb(f"y_ps{h}", [P, BANKS, 512]) for h in range(HALVES)]
        loaded = sem("loaded")
        steps = sem("steps")
        a_done = sem("a_done")
        b_loaded = [sem(f"b_loaded{s}") for s in range(2)]
        c_loaded = [sem(f"c_loaded{s}") for s in range(2)]
        b_used = sem("b_used")
        c_used = sem("c_used")
        decayed = sem("decayed")
        driving = sem("driving")
        driven = sem("driven")
        scanned = sem("scanned")
        read_done = sem("read_done")
        added = sem("added")
        y_done = sem("y_done")
        y_written = sem("y_written")
        y_kept = sem("y_kept")
        block = ctx.enter_context(nc.Block())

        def states(eng, body):
            for s in range(2):
                body(s, s, s == 0, False)
            with eng.Fori(0, STATES // 2 - 2) as i:
                for s in range(2):
                    body(2 * i + 2 + s, s, False, False)
            for s in range(2):
                body(STATES - 2 + s, s, False, s == 1)

        @block.sync
        def _(sp):
            sp.dma_start(a_log[:], d["a_log"]).then_inc(loaded, 16)
            sp.dma_start(skip[:], d["skip"]).then_inc(loaded, 16)
            with sp.Fori(0, CHUNKS) as ch:
                with sp.Fori(0, STATES // 2) as i:
                    for s in range(2):
                        n = 2 * i + s
                        k = ch * STATES + n
                        at = bass.ds(ch * CHUNK, CHUNK)
                        sp.wait_ge(b_used, k + 1)
                        sp.dma_start(b_row[s][:], bc_dram[b, bass.ds(n, 1), at].broadcast_to([P, CHUNK]))\
                            .then_inc(b_loaded[s], 16)
                        sp.wait_ge(c_used, k + 1)
                        sp.dma_start(c_row[s][:], bc_dram[b, bass.ds(n + STATES, 1), at].broadcast_to([P, CHUNK]))\
                            .then_inc(c_loaded[s], 16)

        @block.scalar
        def _(act):
            act.wait_ge(loaded, 32)
            nc.scalar.activation(a_exp[:], a_log[:], ACT.Exp).then_inc(a_done, 1)
            act.wait_ge(a_done, 2)
            with act.Fori(0, CHUNKS) as ch:
                with act.Fori(0, STATES) as n:
                    for h in range(HALVES):
                        u = (ch * STATES + n) * HALVES + h
                        act.wait_ge(scanned, u + 1)
                        nc.scalar.activation(decay[h][:], delta_sb[:, h, bass.ds(ch * CHUNK, CHUNK)], ACT.Exp,
                                             scale=a_sb[:, h, bass.ds(n, 1)]).then_inc(decayed, 1)

        @block.gpsimd
        def _(pool):
            pool.sem_inc(b_used, 2)
            with pool.Fori(0, CHUNKS) as ch:
                with pool.Fori(0, STATES // 2) as i:
                    for s in range(2):
                        k = ch * STATES + 2 * i + s
                        pool.wait_ge(b_loaded[s], (ch * (STATES // 2) + i + 1) * 16)
                        for h in range(HALVES):
                            pool.wait_ge(scanned, k * HALVES + h + 1)
                            pool.sem_inc(driving, 1)
                            nc.gpsimd.tensor_tensor(drive[h][:], du_sb[:, h, bass.ds(ch * CHUNK, CHUNK)],
                                                    b_row[s][:], ALU.mult).then_inc(driven, 1)
                        pool.wait_ge(driven, k * HALVES + HALVES)
                        pool.sem_inc(b_used, 1)

        @block.vector
        def _(dve):
            v = nc.vector
            dve.sem_inc(scanned, 2)
            dve.sem_inc(c_used, 2)
            dve.sem_inc(y_kept, 1)
            v.memset(carry[:], 0.0).then_inc(steps, 1)
            dve.wait_ge(steps, 1)
            dve.wait_ge(a_done, 1)
            v.tensor_scalar(a_sb[:], a_exp[:], -1.0, None, ALU.mult).then_inc(a_done, 1)
            dve.wait_ge(loaded, 32)
            PER = 2 * HALVES
            with dve.Fori(0, CHUNKS) as ch:
                def body(n, s, pair):
                    k = ch * STATES + n
                    own = Tally(dve, steps, k * PER + 1)
                    for h in range(HALVES):
                        u = k * HALVES + h
                        before = carry[:, bass.ds(n, 1), h] if not isinstance(n, int) else carry[:, n, h:h + 1]
                        dve.wait_ge(decayed, u + 1)
                        dve.wait_ge(driven, u + 1)
                        own.done(v.tensor_tensor_scan(out=state[h][:], data0=decay[h][:], data1=drive[h][:],
                                                      initial=before, op0=ALU.mult, op1=ALU.add))
                    for h in range(HALVES):
                        u = k * HALVES + h
                        after = carry[:, bass.ds(n, 1), h] if not isinstance(n, int) else carry[:, n, h:h + 1]
                        dve.wait_ge(steps, own.base + h + 1)
                        dve.sem_inc(scanned, 1)
                        own.done(v.tensor_copy(after, state[h][:, CHUNK - 1:CHUNK]))
                        if h == 0:
                            dve.wait_ge(c_loaded[s], (ch * (STATES // 2) + pair + 1) * 16)
                        dve.wait_ge(added, u + 1)
                        v.tensor_tensor(read[h][s][:], state[h][:], c_row[s][:], ALU.mult).then_inc(read_done, 1)
                    dve.wait_ge(read_done, (k + 1) * HALVES)
                    own.settle()
                    dve.sem_inc(c_used, 1)
                    assert own.n == PER

                for s in range(2):
                    body(s, s, 0)
                with dve.Fori(0, STATES // 2 - 2) as i:
                    for s in range(2):
                        body(2 * i + 2 + s, s, i + 1)
                for s in range(2):
                    body(STATES - 2 + s, s, STATES // 2 - 1)
                dve.wait_ge(y_done, ch + 1)
                at = bass.ds(ch * CHUNK, CHUNK)
                for h in range(HALVES):
                    v.scalar_tensor_tensor(out=y_sb[:, h, at], in0=xs_sb[:, h, at], scalar=skip[:, h:h + 1],
                                           in1=y_ps[h][:].rearrange("p k n -> p (k n)"), op0=ALU.mult,
                                           op1=ALU.add).then_inc(y_written, 1)
                dve.wait_ge(y_written, (ch + 1) * HALVES)
                dve.sem_inc(y_kept, 1)

        @block.tensor
        def _(pe):
            pe.sem_inc(added, 4)
            with pe.Fori(0, CHUNKS) as ch:
                def body(n, s, first, last):
                    k = ch * STATES + n
                    if first:
                        pe.wait_ge(y_kept, ch + 1)
                    for h in range(HALVES):
                        pe.wait_ge(read_done, k * HALVES + h + 1)
                        for q in range(BANKS):
                            m = nc.tensor.matmul(y_ps[h][:, q, :], ident[:], read[h][s][:, q * 512:(q + 1) * 512],
                                                 start=first, stop=last)
                        m.then_inc(added, 1)

                states(pe, body)
                pe.wait_ge(added, (ch + 1) * (STATES * HALVES) + 4)
                pe.sem_inc(y_done, 1)


def gate_and_project(nc, tag, d, b, y_sb, u_dram, gate_dram, x_dram, out_dram):
    with ExitStack() as ctx:
        sb, pb, sem = tools(nc, ctx, tag)
        out_w = sb("out_w", [P, HALVES, P])
        att = [sb(f"att{s}", [P, SPAN]) for s in range(2)]
        z = [sb(f"z{s}", [P, HALVES, SPAN]) for s in range(2)]
        gated = [sb(f"gated{s}", [P, HALVES, SPAN]) for s in range(2)]
        x = [sb(f"x{s}", [P, SPAN]) for s in range(2)]
        out_ps = [pb(f"out_ps{s}", [P, SPAN]) for s in range(2)]
        w_loaded = sem("w_loaded")
        loaded = [sem(f"loaded{s}") for s in range(2)]
        weighed = sem("weighed")
        active = sem("active")
        mixed = sem("mixed")
        product = sem("product")
        summed = sem("summed")
        stored = sem("stored")
        block = ctx.enter_context(nc.Block())
        PER_LOAD = 16 * (2 + HALVES)

        @block.sync
        def _(sp):
            sp.dma_start(out_w[:], d["out_w"]).then_inc(w_loaded, 16)

            def load(c, s):
                at = bass.ds(c * SPAN, SPAN) if not isinstance(c, int) else slice(c * SPAN, (c + 1) * SPAN)
                sp.dma_start(att[s][:], gate_dram[b:b + 1, at].broadcast_to([P, SPAN])).then_inc(loaded[s], 16)
                for h in range(HALVES):
                    sp.dma_start(z[s][:, h, :], u_dram[HALVES + h, b, :, at]).then_inc(loaded[s], 16)
                sp.dma_start(x[s][:], x_dram[b, :, at]).then_inc(loaded[s], 16)

            def store(c, s):
                at = bass.ds(c * SPAN, SPAN) if not isinstance(c, int) else slice(c * SPAN, (c + 1) * SPAN)
                sp.wait_ge(summed, c + 1)
                sp.dma_start(out_dram[b, :, at], x[s][:]).then_inc(stored, 16)
                sp.wait_ge(stored, (c + 1) * 16)

            for s in range(2):
                load(s, s)
            with sp.Fori(0, GPB // 2 - 1) as i:
                for s in range(2):
                    store(2 * i + s, s)
                    load(2 * i + s + 2, s)
            for s in range(2):
                store(GPB - 2 + s, s)

        @block.vector
        def _(dve):
            v = nc.vector
            with dve.Fori(0, GPB // 2) as i:
                for s in range(2):
                    c = 2 * i + s
                    dve.wait_ge(loaded[s], (i + 1) * PER_LOAD)
                    for h in range(HALVES):
                        v.tensor_tensor(z[s][:, h, :], z[s][:, h, :], att[s][:], ALU.mult).then_inc(weighed, 1)
                    dve.wait_ge(active, c + 1)
                    v.tensor_tensor(gated[s][:], z[s][:], y_sb[:, :, bass.ds(c * SPAN, SPAN)],
                                    ALU.mult).then_inc(mixed, 1)
                    dve.wait_ge(product, c + 1)
                    v.tensor_tensor(x[s][:], x[s][:], out_ps[s][:], ALU.add).then_inc(summed, 1)

        @block.scalar
        def _(act):
            with act.Fori(0, GPB // 2) as i:
                for s in range(2):
                    c = 2 * i + s
                    act.wait_ge(weighed, (c + 1) * HALVES)
                    nc.scalar.activation(z[s][:], z[s][:], ACT.Silu).then_inc(active, 1)

        @block.tensor
        def _(pe):
            pe.wait_ge(w_loaded, 16)
            with pe.Fori(0, GPB // 2) as i:
                for s in range(2):
                    c = 2 * i + s
                    pe.wait_ge(mixed, c + 1)
                    for h in range(HALVES):
                        m = nc.tensor.matmul(out_ps[s][:], out_w[:, h, :], gated[s][:, h, :],
                                             start=(h == 0), stop=(h == HALVES - 1))
                    m.then_inc(product, 1)



def layer1_conv(nc, d, ident, x2, x3):
    def scratch(name, shape):
        return nc.dram_tensor(name, shape, F32, kind="Internal").ap()

    u_dram = scratch("u", [ZX, B, P, L])
    zs_dram = scratch("zs", [2, B, L + SPATIAL - 1])
    gate_dram = scratch("gate", [B, L])
    bc_dram = scratch("bc", [B, 2 * STATES, L])
    with ExitStack() as ctx:
        sb, _, _ = tools(nc, ctx, "l1")
        conv1_sb = sb("conv1", [P, HALVES, B, CONV1])
        with ExitStack() as c1:
            sb1, _, _ = tools(nc, c1, "l1a")
            norm_sb = sb1("norm", [P, N])
            total_sb = sb1("total", [P, HALVES, B, GPB])
            peak_sb = sb1("peak", [P, HALVES, B, GPB])
            ztotal_sb = sb1("ztotal", [P, HALVES, TILES])
            zpeak_sb = sb1("zpeak", [P, HALVES, TILES])
            layer_norm(nc, "ln2", ident, x2, None, 1e-6,
                       lambda b, g: norm_sb[:, bass.ds((b * GPB + g) * SPAN, SPAN)])
            project_and_filter(nc, d, ident, norm_sb, u_dram, total_sb, peak_sb, ztotal_sb, zpeak_sb)
            attention(nc, d, ident, total_sb, peak_sb, ztotal_sb, zpeak_sb, conv1_sb, zs_dram, gate_dram)
        for b in range(B):
            sweep(nc)
            with ExitStack() as c1:
                sb1, _, _ = tools(nc, c1, f"l1i{b}")
                y_sb = sb1("y", [P, HALVES, L])
                with ExitStack() as c2:
                    sb2, _, _ = tools(nc, c2, f"l1s{b}")
                    xs_sb = sb2("xs", [P, HALVES, L])
                    causal(nc, f"ca{b}", d, b, u_dram, conv1_sb, xs_sb)
                    delta_sb = sb2("delta", [P, HALVES, L])
                    du_sb = sb2("du", [P, HALVES, L])
                    step_sizes(nc, f"ss{b}", d, b, xs_sb, delta_sb, du_sb, bc_dram)
                    scan(nc, f"sc{b}", d, b, ident, xs_sb, delta_sb, du_sb, y_sb, bc_dram)
                gate_and_project(nc, f"gp{b}", d, b, y_sb, u_dram, gate_dram, x2, x3)
    sweep(nc)


SPECIALISTS = 64
HIDDEN = 512
HCH = HIDDEN // P
EPG = 4
EGROUPS = SPECIALISTS // EPG
WSLOTS = 4


def expert_weights(sp, d, w1, w2, loaded, g, s):
    sp.dma_start(w1[s][:], d["w1"][:, bass.ds(g * EPG, EPG), :]).then_inc(loaded[s], 16)
    sp.dma_start(w2[s][:], d["w2"][:, bass.ds(g * EPG, EPG)]).then_inc(loaded[s], 16)


def choose(nc, d, ident, norm_sb, tok_sb, chosen, pooled_sb, w1, w2, w_loaded):
    with ExitStack() as ctx:
        sb, pb, sem = tools(nc, ctx, "ch")
        gate_w = sb("gate_w", [P, B, P])
        gate_b = sb("gate_b", [P, 1])
        prob = sb("prob", [P, L])
        taken = sb("taken", [P, L])
        best = sb("best", [P, 8])
        peak = sb("peak", [P, 1])
        total = sb("total", [P, 1])
        chosen_tok = [sb(f"chosen_tok{s}", [P, P]) for s in range(2)]
        logit_ps = [pb(f"logit_ps{s}", [P, SPAN]) for s in range(2)]
        turn_ps = [pb(f"turn_ps{s}", [P, 512]) for s in range(2)]
        pool_ps = [pb(f"pool_ps{b}", [P, 512]) for b in range(B)]
        cleared = sem("cleared")
        loaded = sem("loaded")
        product = sem("product")
        kept = sem("kept")
        peaked = sem("peaked")
        exped = sem("exped")
        steps = sem("steps")
        picked = sem("picked")
        turned = sem("turned")
        turn_kept = sem("turn_kept")
        pooled = sem("pooled")
        pooled_kept = sem("pooled_kept")
        block = ctx.enter_context(nc.Block())
        TPI = TILES // B

        @block.gpsimd
        def _(pool):
            nc.gpsimd.memset(gate_w[:], 0.0).then_inc(cleared, 1)

        @block.sync
        def _(sp):
            sp.wait_ge(cleared, 1)
            for b in range(B):
                rows = slice(b * SPECIALISTS, (b + 1) * SPECIALISTS)
                sp.dma_start(gate_w[:, b, rows], d["gate_w"]).then_inc(loaded, 16)
                sp.dma_start(gate_b[rows, :], d["gate_b"]).then_inc(loaded, 16)
            for s in range(WSLOTS):
                expert_weights(sp, d, w1, w2, w_loaded, s, s)

        @block.tensor
        def _(pe):
            pe.wait_ge(loaded, 16 * 2 * B)
            with pe.Fori(0, GPB // 2) as i:
                for s in range(2):
                    c = 2 * i + s
                    pe.wait_ge(kept, c + 1)
                    for b in range(B):
                        m = nc.tensor.matmul(logit_ps[s][:], gate_w[:, b, :],
                                             norm_sb[:, bass.ds(b * L + c * SPAN, SPAN)],
                                             start=(b == 0), stop=(b == B - 1))
                    m.then_inc(product, 1)
            pe.wait_ge(picked, 1)
            for t in range(TPI + 1):
                if t < TPI:
                    if t >= 2:
                        pe.wait_ge(turn_kept, t - 1)
                    nc.tensor.transpose(turn_ps[t % 2][:, 0:P], chosen[:, t * TILE:(t + 1) * TILE],
                                        ident[:]).then_inc(turned, 1)
                if t >= 1:
                    u = t - 1
                    pe.wait_ge(turn_kept, u + 1)
                    for b in range(B):
                        m = nc.tensor.matmul(pool_ps[b][:, 0:SPECIALISTS], tok_sb[:, b * TPI + u, :],
                                             chosen_tok[u % 2][:, b * SPECIALISTS:(b + 1) * SPECIALISTS],
                                             start=(u == 0), stop=(u == TPI - 1))
                    m.then_inc(pooled, 1)

        @block.scalar
        def _(act):
            act.wait_ge(loaded, 16 * 2 * B)
            act.sem_inc(kept, 2)
            with act.Fori(0, GPB // 2) as i:
                for s in range(2):
                    c = 2 * i + s
                    act.wait_ge(product, c + 1)
                    nc.scalar.activation(prob[:, bass.ds(c * SPAN, SPAN)], logit_ps[s][:], ACT.Identity,
                                         bias=gate_b[:]).then_inc(kept, 1)
            act.wait_ge(peaked, 1)
            nc.scalar.activation(prob[:], prob[:], ACT.Exp, bias=peak[:], accum_out=total[:]).then_inc(exped, 1)
            for t in range(TPI):
                act.wait_ge(turned, t + 1)
                if t >= 2:
                    act.wait_ge(pooled, t - 1)
                nc.scalar.activation(chosen_tok[t % 2][:], turn_ps[t % 2][:, 0:P], ACT.Copy).then_inc(turn_kept, 1)
            act.wait_ge(pooled, TPI)
            for b in range(B):
                nc.scalar.activation(pooled_sb[:, b, :], pool_ps[b][:, 0:SPECIALISTS],
                                     ACT.Copy).then_inc(pooled_kept, 1)
            act.wait_ge(pooled_kept, B)

        @block.vector
        def _(dve):
            v = nc.vector
            own = Tally(dve, steps)
            dve.wait_ge(kept, GPB + 2)
            own.done(v.tensor_reduce(peak[:], prob[:], AX_X, ALU.max))
            own.settle()
            v.tensor_scalar(peak[:], peak[:], -1.0, None, ALU.mult).then_inc(peaked, 1)
            dve.wait_ge(exped, 1)
            own.done(v.reciprocal(total[:], total[:]))
            own.settle()
            own.done(v.tensor_scalar(prob[:], prob[:], total[:], None, ALU.mult))
            own.settle()
            own.done(v.max(best[:], prob[:]))
            own.settle()
            own.done(v.match_replace(out=taken[:], in_to_replace=best[:], in_values=prob[:], imm_value=-1.0))
            own.settle()
            v.scalar_tensor_tensor(out=chosen[:], in0=taken[:], scalar=0.0, in1=prob[:], op0=ALU.is_lt,
                                   op1=ALU.mult).then_inc(picked, 1)
            dve.wait_ge(picked, 1)


def specialists(nc, d, ident, pooled_sb, back_sb, w1, w2, w_loaded):
    with ExitStack() as ctx:
        sb, pb, sem = tools(nc, ctx, "sx")
        b1_row = sb("b1_row", [SPECIALISTS, HIDDEN])
        b2_row = sb("b2_row", [SPECIALISTS, P])
        b1 = sb("b1", [P, SPECIALISTS, HCH])
        b2 = sb("b2", [P, SPECIALISTS])
        pre = [sb(f"pre{s}", [P, EPG, HCH, B]) for s in range(2)]
        hid = [sb(f"hid{s}", [P, EPG, HCH, B]) for s in range(2)]
        out_t = sb("out_t", [P, B, SPECIALISTS])
        bias_ps = pb("bias_ps", [P, 512])
        hid_ps = [pb(f"hid_ps{s}", [P, 512]) for s in range(2)]
        out_ps = [pb(f"out_ps{s}", [P, 512]) for s in range(2)]
        back_ps = pb("back_ps", [P, 512])
        rows_loaded = sem("rows_loaded")
        rows_turned = sem("rows_turned")
        b_kept = sem("b_kept")
        first_done = sem("first_done")
        pre_done = sem("pre_done")
        active = sem("active")
        second_done = sem("second_done")
        out_done = sem("out_done")
        cleared = sem("cleared")
        back_turned = sem("back_turned")
        back_kept = sem("back_kept")
        block = ctx.enter_context(nc.Block())

        @block.sync
        def _(sp):
            sp.dma_start(b1_row[:], d["b1"]).then_inc(rows_loaded, 16)
            sp.dma_start(b2_row[:], d["b2"]).then_inc(rows_loaded, 16)
            with sp.Fori(0, EGROUPS // WSLOTS - 1) as i:
                for s in range(WSLOTS):
                    g = (i + 1) * WSLOTS + s
                    sp.wait_ge(second_done, g - WSLOTS + 1)
                    expert_weights(sp, d, w1, w2, w_loaded, g, s)

        @block.tensor
        def _(pe):
            pe.wait_ge(rows_loaded, 32)
            for j in range(HCH):
                nc.tensor.transpose(bias_ps[:, j * SPECIALISTS:(j + 1) * SPECIALISTS],
                                    b1_row[:, j * P:(j + 1) * P], ident[0:SPECIALISTS, 0:SPECIALISTS])
            nc.tensor.transpose(bias_ps[:, HCH * SPECIALISTS:(HCH + 1) * SPECIALISTS], b2_row[:],
                                ident[0:SPECIALISTS, 0:SPECIALISTS]).then_inc(rows_turned, 1)

            def first(g, s, use):
                pe.wait_ge(w_loaded[s], (use + 1) * 32)
                pe.wait_ge(pre_done, g + 1)
                for e in range(EPG):
                    x = pooled_sb[:, :, bass.ds(g * EPG + e, 1)].rearrange("p b e -> p (b e)")
                    for j in range(HCH):
                        at = (e * HCH + j) * B
                        m = nc.tensor.matmul(hid_ps[s % 2][:, at:at + B], w1[s][:, e, j * P:(j + 1) * P], x,
                                             start=True, stop=True)
                m.then_inc(first_done, 1)

            def second(g, s):
                pe.wait_ge(active, g + 1)
                pe.wait_ge(out_done, g + 1)
                for e in range(EPG):
                    for j in range(HCH):
                        m = nc.tensor.matmul(out_ps[s % 2][:, e * B:(e + 1) * B], w2[s][:, e, j, :],
                                             hid[s % 2][:, e, j, :], start=(j == 0), stop=(j == HCH - 1))
                m.then_inc(second_done, 1)

            first(0, 0, 0)
            with pe.Fori(0, EGROUPS // WSLOTS - 1) as i:
                for s in range(WSLOTS):
                    g = i * WSLOTS + s
                    first(g + 1, (s + 1) % WSLOTS, i + (s + 1) // WSLOTS)
                    second(g, s)
            last = EGROUPS // WSLOTS - 1
            for s in range(WSLOTS):
                g = last * WSLOTS + s
                if s + 1 < WSLOTS:
                    first(g + 1, s + 1, last)
                second(g, s)
            pe.wait_ge(out_done, EGROUPS + 2)
            nc.tensor.transpose(back_ps[:, 0:P], out_t[:].rearrange("p b e -> p (b e)"),
                                ident[:]).then_inc(back_turned, 1)

        @block.vector
        def _(dve):
            v = nc.vector
            for b in range(B):
                v.memset(back_sb[b][:], 0.0).then_inc(cleared, 1)
            dve.wait_ge(b_kept, 2)
            dve.sem_inc(pre_done, 2)
            dve.sem_inc(out_done, 2)

            def bias_first(g, s):
                dve.wait_ge(first_done, g + 1)
                bias = b1[:, bass.ds(g * EPG, EPG), :].rearrange("p e j -> p (e j)").unsqueeze(2)\
                    .broadcast_to([P, EPG * HCH, B])
                v.tensor_tensor(pre[s][:].rearrange("p e j b -> p (e j) b"),
                                hid_ps[s][:, 0:EPG * HCH * B].rearrange("p (k b) -> p k b", b=B), bias,
                                ALU.add).then_inc(pre_done, 1)

            def bias_second(g, s):
                dve.wait_ge(second_done, g + 1)
                at = bass.ds(g * EPG, EPG)
                v.tensor_tensor(out_t[:, :, at].rearrange("p b e -> p e b"),
                                out_ps[s][:, 0:EPG * B].rearrange("p (e b) -> p e b", b=B),
                                b2[:, at].unsqueeze(2).broadcast_to([P, EPG, B]), ALU.add).then_inc(out_done, 1)

            bias_first(0, 0)
            with dve.Fori(0, EGROUPS // 2 - 1) as i:
                bias_first(2 * i + 1, 1)
                bias_second(2 * i, 0)
                bias_first(2 * i + 2, 0)
                bias_second(2 * i + 1, 1)
            bias_first(EGROUPS - 1, 1)
            bias_second(EGROUPS - 2, 0)
            bias_second(EGROUPS - 1, 1)

        @block.scalar
        def _(act):
            act.wait_ge(rows_turned, 1)
            nc.scalar.activation(b1[:].rearrange("p e j -> p j e"),
                                 bias_ps[:, 0:HCH * SPECIALISTS].rearrange("p (j e) -> p j e", j=HCH),
                                 ACT.Copy).then_inc(b_kept, 1)
            nc.scalar.activation(b2[:], bias_ps[:, HCH * SPECIALISTS:(HCH + 1) * SPECIALISTS],
                                 ACT.Copy).then_inc(b_kept, 1)
            with act.Fori(0, EGROUPS // 2) as i:
                for s in range(2):
                    g = 2 * i + s
                    act.wait_ge(pre_done, g + 3)
                    nc.scalar.activation(hid[s][:], pre[s][:], ACT.Gelu).then_inc(active, 1)
            act.wait_ge(cleared, B)
            act.wait_ge(back_turned, 1)
            for b in range(B):
                rows = slice(b * SPECIALISTS, (b + 1) * SPECIALISTS)
                nc.scalar.activation(back_sb[b][rows, :], back_ps[rows, 0:P], ACT.Copy).then_inc(back_kept, 1)
            act.wait_ge(back_kept, B)


def give_back(nc, chosen, back_sb, x_dram, out_dram):
    with ExitStack() as ctx:
        sb, pb, sem = tools(nc, ctx, "gb")
        x = [sb(f"x{s}", [P, 2 * SPAN]) for s in range(4)]
        ps = [pb(f"ps{s}", [P, 2, SPAN]) for s in range(4)]
        loaded = [sem(f"loaded{s}") for s in range(4)]
        product = sem("product")
        summed = sem("summed")
        stored = sem("stored")
        block = ctx.enter_context(nc.Block())
        PARTS = L // (2 * SPAN)

        @block.sync
        def _(sp):
            for b in range(B):
                for q in range(PARTS):
                    n = b * PARTS + q
                    at = slice(q * 2 * SPAN, (q + 1) * 2 * SPAN)
                    if n >= 4:
                        m = n - 4
                        sp.wait_ge(summed, m + 1)
                        mb, mq = m // PARTS, m % PARTS
                        sp.dma_start(out_dram[mb, :, mq * 2 * SPAN:(mq + 1) * 2 * SPAN], x[m % 4][:])\
                            .then_inc(stored, 16)
                        sp.wait_ge(stored, 16 * (m + 1))
                    sp.dma_start(x[n % 4][:], x_dram[b, :, at]).then_inc(loaded[n % 4], 16)
            for m in range(B * PARTS - 4, B * PARTS):
                sp.wait_ge(summed, m + 1)
                mb, mq = m // PARTS, m % PARTS
                sp.dma_start(out_dram[mb, :, mq * 2 * SPAN:(mq + 1) * 2 * SPAN], x[m % 4][:]).then_inc(stored, 16)
            sp.wait_ge(stored, 16 * B * PARTS)

        @block.tensor
        def _(pe):
            for b in range(B):
                for q in range(PARTS):
                    n = b * PARTS + q
                    if n >= 4:
                        pe.wait_ge(summed, n - 3)
                    for k in range(2):
                        at = (2 * q + k) * SPAN
                        m = nc.tensor.matmul(ps[n % 4][:, k, :], back_sb[b][:], chosen[:, at:at + SPAN],
                                             start=True, stop=True)
                    m.then_inc(product, 1)

        @block.vector
        def _(dve):
            for n in range(B * PARTS):
                dve.wait_ge(loaded[n % 4], 16 * (n // 4 + 1))
                dve.wait_ge(product, n + 1)
                nc.vector.tensor_tensor(x[n % 4][:], x[n % 4][:], ps[n % 4][:].rearrange("p k n -> p (k n)"),
                                        ALU.add).then_inc(summed, 1)


def layer1_ffn(nc, d, ident, x3, out):
    with ExitStack() as ctx:
        sb, _, sem = tools(nc, ctx, "l1f")
        chosen = sb("chosen", [P, L])
        back_sb = [sb(f"back{b}", [P, P]) for b in range(B)]
        pooled_sb = sb("pooled", [P, B, SPECIALISTS])
        w1 = [sb(f"w1_{s}", [P, EPG, HIDDEN]) for s in range(WSLOTS)]
        w2 = [sb(f"w2_{s}", [P, EPG, HCH, P]) for s in range(WSLOTS)]
        w_loaded = [sem(f"w_loaded{s}") for s in range(WSLOTS)]
        with ExitStack() as c1:
            sb1, _, _ = tools(nc, c1, "l1n")
            norm_sb = sb1("norm", [P, N])
            tok_sb = sb1("tok", [P, TILES, P])
            layer_norm(nc, "ln3", ident, x3, tok_sb, 1e-5,
                       lambda b, g: norm_sb[:, bass.ds((b * GPB + g) * SPAN, SPAN)])
            choose(nc, d, ident, norm_sb, tok_sb, chosen, pooled_sb, w1, w2, w_loaded)
        specialists(nc, d, ident, pooled_sb, back_sb, w1, w2, w_loaded)
        give_back(nc, chosen, back_sb, x3, out)


def build(nc, d, out):
    x1, x2, x3 = [nc.dram_tensor(f"x{n}", [B, P, L], F32, kind="Internal").ap() for n in (1, 2, 3)]
    RETIRED.clear()
    with ExitStack() as ctx:
        sb, _, _ = tools(nc, ctx, "main")
        ident = sb("ident", [P, P])
        make_identity(nc, ident)
        layer0_conv(nc, d, ident, x1)
        layer0_ffn(nc, d, ident, x1, x2)
        layer1_conv(nc, d, ident, x2, x3)
        layer1_ffn(nc, d, ident, x3, out.rearrange("b c h w -> b c (h w)"))


_OUTS = [((B, P, H, W), "float32")]


def conv_columns(offw, modw):
    kk = modw.shape[0]
    off = offw.reshape(kk, 2, *offw.shape[1:])
    return np.ascontiguousarray(np.concatenate([off[:, 0], off[:, 1], modw], 0).transpose(1, 2, 3, 0))


def bias_columns(offb, modb):
    return np.concatenate([offb[0::2], offb[1::2], modb])


def shape_constants():
    token = np.arange(TILE)
    base = np.zeros((P, 2, TAPS), np.float32)
    at = 0
    for _, k in BRANCHES:
        for tap in range(k * k):
            base[:, 0, at] = token // W + tap // k - k // 2
            base[:, 1, at] = token % W + tap % k - k // 2
            at += 1
    rows = np.tile((2.0 * (np.arange(TILES) % (TILES // B))).astype(np.float32), (P, 1))
    return base, rows


def laid_out(i):
    i = {k: np.asarray(v) for k, v in i.items()}
    d = {"x": i["x"].reshape(B, P, L)}
    c = "L0_conv_"
    for name, key in (("b4", "ow4"), ("b3", "ow3"), ("b1", "ow1"), ("b2", "ow2")):
        cols = conv_columns(i[f"{c}{name}_offw"], i[f"{c}{name}_modw"])
        d[key] = cols if cols.shape[1] > 1 else cols[:, 0, 0]
    d["ob"] = np.concatenate([bias_columns(i[f"{c}{n}_offb"], i[f"{c}{n}_modb"]) for n, _ in BRANCHES])[None]
    d["base"], d["rowb"] = shape_constants()
    d["tap_w"] = np.concatenate([i[f"{c}{n}_regw"].reshape(O, P, -1).transpose(1, 2, 0) for n, _ in BRANCHES], 1)
    order = [["b1", "b2", "b3", "b4"].index(n) for n, _ in BRANCHES] + [4]
    fw = i[c + "fuse_w"][:, :, 0, 0].reshape(P, SLOTS_IN, HALVES, P)[:, order]
    d["fuse_w"] = fw.transpose(3, 1, 2, 0).reshape(P, SLOTS_IN * HALVES, P)
    for out, key in (("gn_gamma", "gng"), ("gn_beta", "gnb")):
        g = np.stack([i[f"{c}{n}_{key}"] for n, _ in BRANCHES] + [i[f"{c}pool_{key}"]])
        g = g.reshape(SLOTS_IN * HALVES, P).T
        d[out] = np.concatenate([g] * B, 1)
    d["fuse_gamma"] = np.stack([i[c + "fuse_gng"]] * B, 1)
    d["fuse_beta"] = np.stack([i[c + "fuse_gnb"]] * B, 1)
    d["pool_w"] = i[c + "pool_w"][:, :, 0, 0].T
    at = np.arange(P)
    for name, size in (("average16", O // 16), ("average8", P // 16)):
        d[name] = ((at[:, None] // size == at[None] // size) / size).astype(np.float32)
    f = "L0_ffn_"
    d["expert_w"] = i[f + "expert_w"].transpose(1, 0, 2).reshape(P, EXPERTS * P)
    d["expert_b"] = i[f + "expert_b"]
    d["router_w"] = i[f + "router_w"]
    d["router_b"] = i[f + "router_b"][None]
    d["expert_number"] = np.tile(np.arange(EXPERTS, dtype=np.float32), (P, 1))
    m = "L1_conv_"

    def halves(a):
        return a.reshape(HALVES, P, *a.shape[1:]).swapaxes(0, 1)

    d["in_w"] = i[m + "in_proj_w"].T
    d["dw_w"] = i[m + "dwconv_w"].reshape(ZX, P, DWK * DWK).transpose(1, 0, 2)
    d["fc1"] = halves(i[m + "ca_fc1_w"].T)
    d["fc2"] = i[m + "ca_fc2_w"].T
    d["conv1_w"] = halves(i[m + "conv1d_w"][:, 0])
    d["conv1_b"] = halves(i[m + "conv1d_b"])
    d["spatial_w"] = i[m + "sa_conv_w"].reshape(2 * SPATIAL)
    d["xproj"] = halves(i[m + "x_proj_w"].T)
    d["dtproj"] = i[m + "dt_proj_w"].T
    d["dt_b"] = halves(i[m + "dt_proj_b"])
    d["a_log"] = halves(i[m + "A_log"])
    d["skip"] = halves(i[m + "D"])
    d["out_w"] = halves(i[m + "out_proj_w"].T)
    e = "L1_ffn_"
    d["gate_w"] = i[e + "gate_w"].T
    d["gate_b"] = i[e + "gate_b"][:, None]
    d["w1"] = i[e + "weight1"][:, :P].transpose(1, 0, 2)
    d["b1"] = i[e + "weight1"][:, P]
    d["w2"] = i[e + "weight2"][:, :HIDDEN].reshape(SPECIALISTS, HCH, P, P).transpose(2, 0, 1, 3)
    d["b2"] = i[e + "weight2"][:, HIDDEN]
    return d


def kernel(**inputs):
    import concourse.bacc as _bacc
    from concourse.bass_utils import run_bass_kernel_spmd as _run

    nc = _bacc.Bacc("TRN2", target_bir_lowering=False, num_devices=1)
    arrays, d = {}, {}
    for name, a in laid_out(inputs).items():
        a = np.ascontiguousarray(a)
        arrays[f"in_{name}_dram"] = a
        d[name] = nc.dram_tensor(f"in_{name}_dram", a.shape, mybir.dt.from_np(a.dtype), kind="ExternalInput").ap()
    outs = [nc.dram_tensor(f"out_{i}_dram", shape, mybir.dt.from_np(np.dtype(dtype)), kind="ExternalOutput").ap()
            for i, (shape, dtype) in enumerate(_OUTS)]
    build(nc, d, outs if len(outs) > 1 else outs[0])
    r = _run(nc, [arrays], core_ids=[0])
    got = tuple(r.results[0][f"out_{i}_dram"] for i in range(len(_OUTS)))
    return got if len(got) > 1 else got[0]
```
